# Optimizing a Trainium2 kernel written in Bass

```python
import numpy as np
import jax
import jax.numpy as jnp

def _softmax(x, axis=-1):
    return jax.nn.softmax(x, axis=axis)

def _gelu(x):
    return jax.nn.gelu(x, approximate=True)

def _silu(x):
    return jax.nn.silu(x)

def _sigmoid(x):
    return jax.nn.sigmoid(x)

def _layernorm(x, axis=-1, eps=1e-05):
    m = jnp.mean(x, axis=axis, keepdims=True)
    v = jnp.var(x, axis=axis, keepdims=True)
    return (x - m) / jnp.sqrt(v + eps)

def _scatter_add(tgt, idx, src, axis=0):
    return tgt.at[idx].add(src)

def _segment_sum(src, seg, n):
    return jax.ops.segment_sum(src, seg, n)
kernel_name = 'mk_decoder_postln_d1_seqx_r4_3beff7'

def setup_inputs(seed: int=0):
    np.random.seed(seed)
    _w = jnp.asarray

    def _rec_inputs():
        import jax
        import jax.numpy as jnp
        _rk = jax.random.key(seed)
        x = -7.109e-05 + 0.9999 * jax.random.normal(jax.random.fold_in(_rk, 1), (2, 512, 1024), jnp.float32)
        _lenS = 512 - jax.random.randint(jax.random.fold_in(_rk, 7), (2,), 0, max(1, 512 // 4) + 1, jnp.int32)
        _lenS2 = 1024 - jax.random.randint(jax.random.fold_in(_rk, 8), (2,), 0, max(1, 1024 // 4) + 1, jnp.int32)
        _ctx_4096P = jax.random.normal(jax.random.fold_in(_rk, 11), (2, 16, 1024), jnp.float32)
        _ctx_4096c = jax.random.dirichlet(jax.random.fold_in(_rk, 511), 0.3 * jnp.ones((16,), jnp.float32), (2, 1024))
        _ctx_4096t = jnp.einsum('bsk,bkd->bsd', _ctx_4096c, _ctx_4096P)
        _ctx_4096t = _ctx_4096t * jax.lax.rsqrt(jnp.mean(jnp.square(_ctx_4096t)) + 1e-12) * 0.953939
        ctx_4096 = -2.6191e-05 + 0.999952 * (_ctx_4096t + 0.3 * jax.random.normal(jax.random.fold_in(_rk, 611), (2, 1024, 1024), jnp.float32))
        return (x, ctx_4096)
    x, ctx_4096 = _rec_inputs()

    def _L0_attn_setup():
        import math
        import jax, jax.numpy as jnp
        import numpy as np
        N_HEADS = 32
        ALIBI_BIAS_MAX = 8

        def _alibi_slopes(n_heads, alibi_bias_max=8):
            _n = 2 ** math.ceil(math.log2(n_heads))
            m = jnp.arange(1, _n + 1, dtype=jnp.float32) * (alibi_bias_max / _n)
            slopes = 1.0 / jnp.power(2.0, m)
            if _n != n_heads:
                slopes = jnp.concatenate([slopes[1::2], slopes[::2]])[:n_heads]
            return slopes
        key = jax.random.key(seed)
        k1, k2, k3 = jax.random.split(key, 3)
        B, S, D = (1, 512, 1024)
        x = jax.random.normal(k1, (B, S, D), dtype=jnp.float32)
        w_qkv = jax.random.normal(k2, (3 * D, D), dtype=jnp.float32) * 0.02
        b_qkv = jnp.zeros((3 * D,), dtype=jnp.float32)
        w_out = jax.random.normal(k3, (D, D), dtype=jnp.float32) * 0.02
        b_out = jnp.zeros((D,), dtype=jnp.float32)
        return {'x': x, 'w_qkv': w_qkv, 'b_qkv': b_qkv, 'w_out': w_out, 'b_out': b_out}
    _L0_attn_all = _L0_attn_setup()
    _L0_attn_in = {k: v for k, v in _L0_attn_all.items() if k in ('w_qkv', 'b_qkv', 'w_out', 'b_out')}
    del _L0_attn_all

    def _L0_xattn_setup():
        import jax, jax.numpy as jnp
        import numpy as np
        TEXT_DIM = 1024
        FEATURE_DIM = 1024

        def _xavier_uniform(key, shape):
            fan_in, fan_out = (shape[1], shape[0])
            limit = float(np.sqrt(6.0 / (fan_in + fan_out)))
            return jax.random.uniform(key, shape, jnp.float32, -limit, limit)
        key = jax.random.key(seed)
        k1, k2, k3, k4 = jax.random.split(key, 4)
        text = jax.random.normal(k1, (8, 512, TEXT_DIM), jnp.float32)
        features = jax.random.normal(k2, (8, 144, FEATURE_DIM), jnp.float32)
        Wq = _xavier_uniform(k3, (FEATURE_DIM, TEXT_DIM))
        bq = jnp.zeros((FEATURE_DIM,), jnp.float32)
        Wk = _xavier_uniform(k4, (FEATURE_DIM, FEATURE_DIM))
        bk = jnp.zeros((FEATURE_DIM,), jnp.float32)
        return {'text': text, 'features': features, 'Wq': Wq, 'bq': bq, 'Wk': Wk, 'bk': bk}
    _L0_xattn_all = _L0_xattn_setup()
    _L0_xattn_in = {k: v for k, v in _L0_xattn_all.items() if k in ('Wq', 'bq', 'Wk', 'bk')}
    del _L0_xattn_all

    def _L0_ffn_setup():
        import jax, jax.numpy as jnp
        import numpy as np
        HD, M = (1024, 3584)
        key = jax.random.key(seed)
        k_x, k_g, k_u, k_d = jax.random.split(key, 4)
        scale = 1.0 / np.sqrt(HD)
        x = jax.random.normal(k_x, (4, 512, HD), dtype=jnp.float16)
        W_gate = jax.random.normal(k_g, (M, HD), dtype=jnp.float16) * jnp.float16(scale)
        W_up = jax.random.normal(k_u, (M, HD), dtype=jnp.float16) * jnp.float16(scale)
        W_down = jax.random.normal(k_d, (HD, M), dtype=jnp.float16) * jnp.float16(1.0 / np.sqrt(M))
        return {'x': x, 'W_gate': W_gate, 'W_up': W_up, 'W_down': W_down}
    _L0_ffn_all = _L0_ffn_setup()
    _L0_ffn_in = {k: v for k, v in _L0_ffn_all.items() if k in ('W_gate', 'W_up', 'W_down')}
    del _L0_ffn_all
    return {'x': x, 'ctx_4096': ctx_4096, 'L0_attn_w_qkv': _L0_attn_in['w_qkv'], 'L0_attn_b_qkv': _L0_attn_in['b_qkv'], 'L0_attn_w_out': _L0_attn_in['w_out'], 'L0_attn_b_out': _L0_attn_in['b_out'], 'L0_xattn_Wq': _L0_xattn_in['Wq'], 'L0_xattn_bq': _L0_xattn_in['bq'], 'L0_xattn_Wk': _L0_xattn_in['Wk'], 'L0_xattn_bk': _L0_xattn_in['bk'], 'L0_ffn_W_gate': _L0_ffn_in['W_gate'], 'L0_ffn_W_up': _L0_ffn_in['W_up'], 'L0_ffn_W_down': _L0_ffn_in['W_down']}

def reference(x, ctx_4096, L0_attn_w_qkv, L0_attn_b_qkv, L0_attn_w_out, L0_attn_b_out, L0_xattn_Wq, L0_xattn_bq, L0_xattn_Wk, L0_xattn_bk, L0_ffn_W_gate, L0_ffn_W_up, L0_ffn_W_down):
    import jax
    import jax.numpy as jnp

    def _L0_attn_ref(x, w_qkv, b_qkv, w_out, b_out):
        import math
        import jax, jax.numpy as jnp
        import numpy as np
        N_HEADS = 32
        ALIBI_BIAS_MAX = 8

        def _alibi_slopes(n_heads, alibi_bias_max=8):
            _n = 2 ** math.ceil(math.log2(n_heads))
            m = jnp.arange(1, _n + 1, dtype=jnp.float32) * (alibi_bias_max / _n)
            slopes = 1.0 / jnp.power(2.0, m)
            if _n != n_heads:
                slopes = jnp.concatenate([slopes[1::2], slopes[::2]])[:n_heads]
            return slopes
        B, S, D = x.shape
        H = N_HEADS
        hd = D // H
        qkv = jnp.einsum('bsd,od->bso', x, w_qkv) + b_qkv
        q, k, v = jnp.split(qkv, 3, axis=-1)
        q = q.reshape(B, S, H, hd)
        k = k.reshape(B, S, H, hd)
        v = v.reshape(B, S, H, hd)
        scale = 1.0 / math.sqrt(hd)
        scores = jnp.einsum('bqhd,bkhd->bhqk', q, k) * scale
        slopes = _alibi_slopes(H, ALIBI_BIAS_MAX)
        positions = jnp.arange(1 - S, 1, dtype=jnp.float32)
        alibi = slopes[:, None] * positions[None, :]
        scores = scores + alibi[None, :, None, :]
        causal = jnp.arange(S)[:, None] >= jnp.arange(S)[None, :]
        scores = jnp.where(causal[None, None, :, :], scores, jnp.float32(-1000000000.0))
        attn = jax.nn.softmax(scores, axis=-1)
        out = jnp.einsum('bhqk,bkhd->bqhd', attn, v).reshape(B, S, D)
        return jnp.einsum('bsd,od->bso', out, w_out) + b_out

    def _L0_xattn_ref(text, features, Wq, bq, Wk, bk):
        import jax, jax.numpy as jnp
        import numpy as np
        TEXT_DIM = 1024
        FEATURE_DIM = 1024

        def _xavier_uniform(key, shape):
            fan_in, fan_out = (shape[1], shape[0])
            limit = float(np.sqrt(6.0 / (fan_in + fan_out)))
            return jax.random.uniform(key, shape, jnp.float32, -limit, limit)
        Q = jnp.einsum('btx,dx->btd', text, Wq) + bq
        K = jnp.einsum('bpx,dx->bpd', features, Wk) + bk
        scale = 1.0 / jnp.sqrt(jnp.asarray(K.shape[-1], K.dtype))
        scores = jnp.einsum('btd,bpd->btp', Q, K) * scale
        attn = jax.nn.softmax(scores, axis=-1)
        attended = jnp.einsum('btp,bpd->btd', attn, features)
        return attended

    def _L0_ffn_ref(x, W_gate, W_up, W_down):
        import jax, jax.numpy as jnp
        import numpy as np
        HD, M = (1024, 3584)
        gate = jnp.einsum('bsh,mh->bsm', x, W_gate)
        up = jnp.einsum('bsh,mh->bsm', x, W_up)
        h = jax.nn.silu(gate) * up
        out = jnp.einsum('bsm,hm->bsh', h, W_down)
        return out
    x = _layernorm(x + _L0_attn_ref(x, L0_attn_w_qkv, L0_attn_b_qkv, L0_attn_w_out, L0_attn_b_out), axis=-1)
    x = _layernorm(x + _L0_xattn_ref(x, ctx_4096, L0_xattn_Wq, L0_xattn_bq, L0_xattn_Wk, L0_xattn_bk), axis=-1)
    x = _layernorm(x + _L0_ffn_ref(x, L0_ffn_W_gate, L0_ffn_W_up, L0_ffn_W_down), axis=-1)
    return x

_drawn_inputs = setup_inputs


def setup_inputs(seed=0):
    import zlib

    import numpy as np

    out = dict(_drawn_inputs(seed))
    spreads = {'L0_attn_b_qkv': (0.0, 0.1),
     'L0_attn_b_out': (0.0, 0.1),
     'L0_xattn_bq': (0.0, 0.378),
     'L0_xattn_bk': (0.0, 0.8)}
    factors = {}
    for name, (base, spread) in spreads.items():
        noise = np.random.default_rng([zlib.crc32(name.encode()), seed]).standard_normal(out[name].shape)
        drawn = base * np.exp(spread * noise) if base else spread * noise
        out[name] = jnp.asarray(drawn.astype(out[name].dtype))
    for name, factor in factors.items():
        out[name] = (out[name] * factor).astype(out[name].dtype)
    return out
```

```python
import concourse.bass as bass
from concourse import mybir
from contextlib import ExitStack

B, T, D = 2, 512, 1024
H, HD = 32, 32
F = 3584
P = 128
C = D // P
TB = T // P
HG = P // HD
NG = H // HG
UNITS = B * NG
HEADS = UNITS * HG
MB = F // P
BANK = 512
HALVES = D // BANK
EPS = 1e-5
ALIBI_MAX = 8
PROB_UP = 2.0 ** 15
FP16_UP = 1024.0

PIECES = ((3,), (2, 0), (1,))
BLOCK_AT, PIECE_AT, HEAD_COLS = {}, [], 0
for _piece in PIECES:
    _first = HEAD_COLS
    for _i in _piece:
        BLOCK_AT[_i] = HEAD_COLS
        HEAD_COLS += P * (_i + 1)
    PIECE_AT.append((_first, HEAD_COLS))

HI, LO = 0, 1
PAIRS = ((HI, HI), (HI, LO), (LO, HI))

IDENT, RAMP, TRI, SLOPE = 0, P, P + T, P + T + P
CONSTS = SLOPE + HEADS
MASKED = -3e38


def wait(engine, semaphore, count):
    if not (isinstance(count, int) and count <= 0):
        engine.wait_ge(semaphore, count)


def attention(nc, sem, place, at, at_rest, consts, qkv_bias, x_half, dense_fetch, dram):
    fp32, fp32r = mybir.dt.float32, mybir.dt.float32r
    fp16, bf16 = mybir.dt.float16, mybir.dt.bfloat16
    ALU, ACT = mybir.AluOpType, mybir.ActivationFunctionType
    scale = float(HD) ** -0.5
    XR = 4
    Q, K, V = range(3)
    VP = 3

    def sb(name, shape, dtype):
        nonlocal at
        t, at = place(name, shape, dtype, at)
        return t

    x_raw = sb("x_raw", [P, XR, T], fp32)
    w_raw = sb("w_raw", [P, 3, C, P], fp32)
    w_half = [sb("w_hi", [P, 3, C, P], fp32r), None]
    at = at_rest
    w_half[LO] = sb("w_lo", [P, 3, C, P], fp32r)
    qk = sb("qk", [P, 4, T], fp32r)
    stack = sb("stack", [P, 2, HG, 2, T], fp32r)
    v_t = sb("v_t", [P, T], fp32)
    v = sb("v", [P, 2, TB, HG, VP, HD], bf16)
    v_rest = sb("v_rest", [P, TB, HG, HD], fp32)
    bias_tile = sb("bias_tile", [P, 2, T], fp32)
    probs = sb("probs", [P, 2, HEAD_COLS], fp32)
    pt_half = [sb("pt_hi", [P, 2, HEAD_COLS], fp16), sb("pt_lo", [P, 2, HEAD_COLS], fp16)]
    top = sb("top", [P, 2, TB], fp32)
    neg_top = sb("neg_top", [P, 2, TB], fp32)
    sums = sb("sums", [P, 2, HG, TB], fp32)
    inv_sums = sb("inv_sums", [P, 2, TB], fp32)
    o_sum = sb("o_sum", [P, 2, TB, HD], fp32)
    att = sb("att", [P, TB, HG, HD], fp32)
    att_t = sb("att_t", [P, T], fp32)
    zero = sb("zero", [P, 1], fp32)
    ident = consts[:, IDENT:IDENT + P]

    consts_in = sem("consts_in")
    x_in = [sem(f"x_in{k}") for k in range(XR)]
    x_hi_done = sem("x_hi_done")
    x_done = sem("x_done")
    w_in = [sem(f"w_in{k}") for k in range(3)]
    w_hi_done = sem("w_hi_done")
    w_done = sem("w_done")
    proj_done = sem("proj_done")
    qk_hi_done = sem("qk_hi_done")
    qk_done = sem("qk_done")
    stacked = [sem(f"stacked{j}") for j in range(HG)]
    v_t_done = sem("v_t_done")
    v_flipped = sem("v_flipped")
    v_first_done = sem("v_first_done")
    v_rest_done = sem("v_rest_done")
    v_second_done = sem("v_second_done")
    v_done = sem("v_done")
    ramp_done = sem("ramp_done")
    bias_done = sem("bias_done")
    scored = sem("scored")
    biased = sem("biased")
    top_done = sem("top_done")
    exp_done = sem("exp_done")
    flipped = sem("flipped")
    pt_hi_done = sem("pt_hi_done")
    pt_done = sem("pt_done")
    o_done = sem("o_done")
    o_sum_done = sem("o_sum_done")
    inv_done = sem("inv_done")
    att_done = sem("att_done")
    att_flipped = sem("att_flipped")
    att_t_done = sem("att_t_done")
    att_stored = dense_fetch.att_stored
    biasing = sem("biasing")
    zero_done = sem("zero_done")

    LOOPS = ((2, NG, 0), (NG, UNITS - 2, 1))

    def steps(engine, step):
        for s in (0, 1):
            step(s, s, 0)
        for first, end, batch in LOOPS:
            with engine.Fori(0, (end - first) // 2) as i:
                step(i * 2 + first, 0, batch)
                step(i * 2 + (first + 1), 1, batch)
        for s in range(UNITS - 2, UNITS + 2):
            step(s, s % 2, 1)

    def has(s, unit_of_step):
        return not isinstance(s, int) or 0 <= s + unit_of_step < UNITS

    def settled(engine):
        engine.wait_ge(consts_in, 16)

    with ExitStack() as scope:
        def bank(name):
            return scope.enter_context(nc.psum_tensor(name, [P, BANK], fp32))

        proj = [bank("proj0"), bank("proj1")]
        score = [bank("score0"), bank("score1"), None]
        flip = [bank("flip0"), bank("flip1"), None]
        score[2], flip[2] = score[0], flip[0]
        o_ps = bank("o_ps")
        misc = bank("misc")
        o_parts = o_ps[:, 0:TB * VP * HD].rearrange("p (b x c) -> p b c x", b=TB, x=VP)
        misc_v = misc[:, :].rearrange("p (b h c) -> p b h c", b=TB, h=HG)

        block = scope.enter_context(nc.Block())

        @block.sync
        def _(sp):
            def load_x(n):
                wait(sp, x_done, n - XR + 1)
                sp.dma_start(x_raw[:, n % XR, :], dram["x_t"][n // C, n % C, :, :]).then_inc(x_in[n % XR], 16)

            def load_w(u, kind):
                wait(sp, w_done, (u - 1) * 3 + kind + 1)
                source = dram["wqkv"][bass.ds((u % NG) * 3 + kind, 1), :, :].rearrange("a p n -> p (a n)")
                sp.dma_start(w_raw[:, kind, :, :].rearrange("p c n -> p (c n)"), source).then_inc(w_in[kind], 16)

            load_w(0, Q)
            for n in range(XR):
                load_x(n)
            sp.dma_start(consts[:, :], dram["consts"]).then_inc(consts_in, 16)
            load_w(0, K)
            load_w(0, V)
            for n in range(XR, C):
                load_x(n)
            sp.dma_start(qkv_bias[:, :], dram["qkv_bias"]).then_inc(consts_in, 16)
            load_w(1, Q)
            for n in range(C, C + XR):
                load_x(n)
            load_w(1, K)

            def step(s, par, batch):
                if isinstance(s, int) and s == 1:
                    for n in range(C + XR, B * C):
                        load_x(n)
                if has(s, 1):
                    load_w(s + 1, V)
                if has(s, 2):
                    load_w(s + 2, Q)
                if has(s, 0):
                    wait(sp, qk_done, s * 2 + 2)
                    wait(sp, scored, (s - 1) * HG * 3)
                    for j in range(HG):
                        for r in range(4):
                            a, b = r // 2, 2 + r % 2
                            rows, to = slice(HD * j, HD * j + HD), slice(HD * r, HD * r + HD)
                            sp.dma_start(stack[to, par, j, :, :].bitcast(fp32),
                                         qk[rows, a:b + 1:b - a, :].bitcast(fp32)).then_inc(stacked[j], 16)
                if has(s, 2):
                    load_w(s + 2, K)
                if isinstance(s, int) and s == UNITS + 1:
                    sp.wait_ge(att_stored, 16 * (UNITS - 1))
                    sp.wait_ge(proj_done, 3 * UNITS)
                    dense_fetch.start(sp)
                if has(s, -2):
                    wait(sp, att_t_done, s - 1)
                    target = dram["att_t"][bass.ds(s - 2, 1), :, :].rearrange("a p n -> p (a n)")
                    sp.dma_start(target, att_t[:, :]).then_inc(att_stored, 16)

            steps(sp, step)

        @block.gpsimd
        def _(pool):
            def split_w(u, kind):
                pool.wait_ge(w_hi_done, u * 3 + kind + 1)
                nc.gpsimd.tensor_tensor(w_half[LO][:, kind, :, :], w_raw[:, kind, :, :],
                                        w_half[HI][:, kind, :, :].bitcast(fp32), ALU.subtract).then_inc(w_done, 1)

            def make_bias(h, slot):
                wait(pool, biased, (h - 1) * 3)
                settled(pool)
                nc.gpsimd.tensor_tensor(bias_tile[:, slot, :], consts[:, RAMP:RAMP + T],
                                        consts[:, bass.ds(h + SLOPE, 1)].broadcast_to([P, T]),
                                        ALU.mult).then_inc(ramp_done, 1)
                pool.wait_ge(ramp_done, h + 1)
                nc.gpsimd.tensor_tensor(bias_tile[:, slot, T - P:T], bias_tile[:, slot, T - P:T],
                                        consts[:, TRI:TRI + P], ALU.add).then_inc(bias_done, 1)

            split_w(0, K)
            split_w(0, V)

            def step(s, par, batch):
                if has(s, 0) and not (isinstance(s, int) and s == 0):
                    split_w(s, V)
                if has(s, -1):
                    pool.wait_ge(v_second_done, s)
                    nc.gpsimd.tensor_tensor(v[:, 1 - par, :, :, 2, :], v_rest[:, :, :, :],
                                            v[:, 1 - par, :, :, 1, :], ALU.subtract).then_inc(v_done, 1)
                if has(s, -1):
                    for j in range(1, HG):
                        make_bias((s - 1) * HG + j, j % 2)
                if has(s, 1):
                    split_w(s + 1, Q)
                if has(s, 0):
                    make_bias(s * HG, 0)
                if has(s, 1):
                    split_w(s + 1, K)

            steps(pool, step)

        @block.scalar
        def _(act):
            def split_w(u, kind):
                act.wait_ge(w_in[kind], u * 16 + 16)
                wait(act, proj_done, (u - 1) * 3 + kind + 1)
                nc.scalar.activation(w_half[HI][:, kind, :, :], w_raw[:, kind, :, :], ACT.Copy).then_inc(w_hi_done, 1)

            def split_x(n):
                act.wait_ge(x_in[n % XR], n // XR * 16 + 16)
                nc.scalar.activation(x_half[HI][:, n // C, n % C, :], x_raw[:, n % XR, :], ACT.Copy).then_inc(x_hi_done, 1)

            def bias_of(u, kind):
                return qkv_bias[:, bass.ds(u + kind * UNITS, 1)]

            act.wait_ge(zero_done, 1)
            nc.scalar.activation(zero[:, :], zero[:, :], ACT.Exp, bias=0.0, scale=0.0)
            split_w(0, Q)
            for n in range(XR):
                split_x(n)
            split_w(0, K)
            for n in range(XR, C):
                split_x(n)
            split_w(0, V)
            act.wait_ge(consts_in, 32)

            def step(s, par, batch):
                for j in range(HG):
                    if isinstance(s, int) and s == 1:
                        split_x(C + 2 * j)
                        split_x(C + 2 * j + 1)
                    if isinstance(s, int) and s == UNITS + 1 and j == 1:
                        nc.scalar.activation(zero[:, :], zero[:, :], ACT.Sqrt, bias=0.0, scale=0.0)
                    if j == 0 and has(s, -1):
                        act.wait_ge(proj_done, s * 3)
                        wait(act, v_flipped, s - 1)
                        settled(act)
                        nc.scalar.activation(v_t[:, :], proj[1 - par][:, :], ACT.Identity,
                                             bias=bias_of(s - 1, V)).then_inc(v_t_done, 1)
                    if j == 0 and has(s, 0) and not (isinstance(s, int) and s == 0):
                        split_w(s, V)
                    if j == 3 and has(s, -2):
                        act.wait_ge(att_flipped, s - 1)
                        wait(act, att_stored, (s - 2) * 16)
                        nc.scalar.activation(att_t[:, :], misc[:, :], ACT.Copy, scale=1.0 / PROB_UP).then_inc(att_t_done, 1)
                    if has(s, -1 if j else -2):
                        h = (s - 1) * HG + j - 1
                        for k, (lo, hi) in enumerate(PIECE_AT):
                            act.wait_ge(flipped, h * 3 + k + 1)
                            if k == 0:
                                wait(act, o_done, h - 1)
                            nc.scalar.activation(pt_half[HI][:, (j - 1) % 2, lo:hi], flip[k][:, 0:hi - lo],
                                                 ACT.Copy, scale=PROB_UP).then_inc(pt_hi_done, 1)
                            if k == 0 and j == 1 and has(s, 0):
                                qk_hi(s, Q)
                            if k == 1 and j == 0 and has(s, -1):
                                v_first(s, par)
                            if k == 2 and j == 0 and has(s, -1):
                                v_second(s, par)
                    else:
                        if j == 1 and has(s, 0):
                            qk_hi(s, Q)
                        if j == 0 and has(s, -1):
                            v_first(s, par)
                            v_second(s, par)
                    if j == 2 and has(s, 0):
                        qk_hi(s, K)
                    if j == 2 and has(s, 1):
                        split_w(s + 1, Q)
                    if j == 3 and has(s, 1):
                        split_w(s + 1, K)
                    if has(s, -1):
                        h = (s - 1) * HG + j
                        act.wait_ge(top_done, h + 1)
                        if j == 0:
                            wait(act, inv_done, (s - 2) * 2)
                        for i in (3, 2, 0, 1):
                            cols = probs[:, j % 2, BLOCK_AT[i]:BLOCK_AT[i] + P * (i + 1)]
                            last = nc.scalar.activation(cols, cols, ACT.Exp, bias=neg_top[:, j % 2, i:i + 1],
                                                        scale=scale, accum_out=sums[:, 1 - par, j, i:i + 1])
                        last.then_inc(exp_done, 1)

            def v_first(s, par):
                act.wait_ge(v_flipped, s)
                wait(act, o_done, (s - 2) * HG)
                nc.scalar.activation(v[:, 1 - par, :, :, 0, :], misc_v, ACT.Copy).then_inc(v_first_done, 1)

            def v_second(s, par):
                act.wait_ge(v_rest_done, s)
                nc.scalar.activation(v[:, 1 - par, :, :, 1, :], v_rest[:, :, :, :], ACT.Copy).then_inc(v_second_done, 1)

            def qk_hi(s, kind):
                act.wait_ge(proj_done, s * 3 + kind + 1)
                if kind == Q:
                    for j in range(HG):
                        wait(act, stacked[j], s * 64)
                settled(act)
                nc.scalar.activation(qk[:, 2 * kind, :], proj[(par_of(s) + kind) % 2][:, :], ACT.Identity,
                                     bias=bias_of(s, kind)).then_inc(qk_hi_done, 1)

            current = [0]

            def par_of(s):
                return current[0]

            def step_with_parity(s, par, batch):
                current[0] = par
                step(s, par, batch)

            steps(act, step_with_parity)

        @block.vector
        def _(dve):
            def split_x(n):
                dve.wait_ge(x_hi_done, n + 1)
                nc.vector.tensor_tensor(x_half[LO][:, n // C, n % C, :], x_raw[:, n % XR, :],
                                        x_half[HI][:, n // C, n % C, :].bitcast(fp32), ALU.subtract).then_inc(x_done, 1)

            nc.vector.memset(zero[:, :], 0.0).then_inc(zero_done, 1)
            dve.wait_ge(w_hi_done, 1)
            nc.vector.tensor_tensor(w_half[LO][:, Q, :, :], w_raw[:, Q, :, :],
                                    w_half[HI][:, Q, :, :].bitcast(fp32), ALU.subtract).then_inc(w_done, 1)
            for n in range(C):
                split_x(n)
            dve.wait_ge(consts_in, 32)

            def bias_scores(h, j, k):
                if k == 0:
                    dve.wait_ge(bias_done, h + 1)
                    wait(dve, flipped, (h - 1) * 3)
                dve.wait_ge(scored, h * 3 + k + 1)
                dve.sem_inc(biasing, 1)
                for i in PIECES[k]:
                    lo, width = BLOCK_AT[i], P * (i + 1)
                    first = lo - PIECE_AT[k][0]
                    last = nc.vector.tensor_tensor_reduce(
                        out=probs[:, j % 2, lo:lo + width], in0=score[k][:, first:first + width],
                        in1=bias_tile[:, j % 2, T - width:T], scale=1.0, scalar=MASKED,
                        op0=ALU.add, op1=ALU.max, accum_out=top[:, j % 2, i:i + 1])
                last.then_inc(biased, 1)

            def pt_lo(h, j, k):
                lo, hi = PIECE_AT[k]
                dve.wait_ge(pt_hi_done, h * 3 + k + 1)
                nc.vector.scalar_tensor_tensor(out=pt_half[LO][:, (j - 1) % 2, lo:hi], in0=flip[k][:, 0:hi - lo],
                                               scalar=PROB_UP, in1=pt_half[HI][:, (j - 1) % 2, lo:hi],
                                               op0=ALU.mult, op1=ALU.subtract).then_inc(pt_done, 1)

            def qk_lo(s, par, kind):
                dve.wait_ge(qk_hi_done, s * 2 + kind + 1)
                nc.vector.scalar_tensor_tensor(out=qk[:, 2 * kind + 1, :], in0=proj[(par + kind) % 2][:, :],
                                               scalar=qkv_bias[:, bass.ds(s + kind * UNITS, 1)],
                                               in1=qk[:, 2 * kind, :].bitcast(fp32),
                                               op0=ALU.add, op1=ALU.subtract).then_inc(qk_done, 1)

            def step(s, par, batch):
                for j in range(HG):
                    if isinstance(s, int) and s == 1:
                        split_x(C + 2 * j)
                        split_x(C + 2 * j + 1)
                    if has(s, -1 if j == 3 else -2):
                        head = (j - 3) % HG
                        dve.wait_ge(o_done, (s - 1) * HG + j - 2)
                        if head % 2 == 0:
                            wait(dve, att_done, ((s - 1) if j == 3 else (s - 2)) * 2 + head // 2)
                        nc.vector.tensor_reduce(o_sum[:, head % 2, :, :], o_parts, mybir.AxisListType.X,
                                                ALU.add).then_inc(o_sum_done, 1)
                    if j in (0, 2) and has(s, -2):
                        pair = (s - 2) * 2 + j // 2
                        nc.vector.reciprocal(inv_sums[:, :, :], sums[:, par, j:j + 2, :]).then_inc(inv_done, 1)
                        wait(dve, att_flipped, s - 2)
                        dve.wait_ge(inv_done, pair + 1)
                        dve.wait_ge(o_sum_done, pair * 2 + 2)
                        nc.vector.tensor_tensor(
                            att[:, :, j:j + 2, :], o_sum[:, :, :, :].rearrange("p h b c -> p b h c"),
                            inv_sums[:, :, :].rearrange("p h b -> p b h").unsqueeze(3).broadcast_to([P, TB, 2, HD]),
                            ALU.mult).then_inc(att_done, 1)
                    scores, flips = has(s, -1), has(s, -1 if j else -2)
                    h = (s - 1) * HG + j
                    if scores:
                        bias_scores(h, j, 0)
                        bias_scores(h, j, 1)
                    if flips:
                        pt_lo(h - 1, j, 0)
                    if j == 1 and has(s, 0):
                        qk_lo(s, par, Q)
                    if flips:
                        pt_lo(h - 1, j, 1)
                    if j == 0 and has(s, -1):
                        dve.wait_ge(v_first_done, s)
                        wait(dve, v_done, s - 1)
                        nc.vector.tensor_tensor(v_rest[:, :, :, :], misc_v, v[:, 1 - par, :, :, 0, :],
                                                ALU.subtract).then_inc(v_rest_done, 1)
                    if scores:
                        bias_scores(h, j, 2)
                        dve.wait_ge(biased, h * 3 + 3)
                        nc.vector.tensor_scalar(neg_top[:, j % 2, :], top[:, j % 2, :], -scale, None,
                                                ALU.mult).then_inc(top_done, 1)
                    if flips:
                        pt_lo(h - 1, j, 2)
                    if j == 2 and has(s, 0):
                        qk_lo(s, par, K)

            steps(dve, step)

        @block.tensor
        def _(pe):
            def project(s, par, batch, products):
                for n in products:
                    kind, c, pair = n // (3 * C), n // 3 % C, n % 3
                    a, b = PAIRS[pair]
                    if n % (3 * C) == 0:
                        pe.wait_ge(w_done, s * 3 + kind + 1)
                        if kind == V:
                            pe.wait_ge(qk_done, s * 2 + 1)
                        else:
                            wait(pe, (qk_done, v_t_done)[kind], (s * 2, s)[kind])
                        if kind == Q and not (isinstance(s, int) and s == 0):
                            pe.wait_ge(x_done, (batch + 1) * C)
                    if isinstance(s, int) and s == 0 and kind == Q and pair == 0:
                        pe.wait_ge(x_done, c + 1)
                    last = nc.tensor.matmul(proj[(par + kind) % 2][:, :], w_half[a][:, kind, c, :],
                                            x_half[b][:, batch, c, :], start=(n % (3 * C) == 0),
                                            stop=(n % (3 * C) == 3 * C - 1))
                    if n % (3 * C) == 3 * C - 1:
                        last.then_inc(proj_done, 1)

            def score_piece(h, j, unit_par, k):
                wait(pe, biased, h * 3 + (1 if k == 2 else 0))
                for i in PIECES[k]:
                    first, width = BLOCK_AT[i] - PIECE_AT[k][0], P * (i + 1)
                    last = nc.tensor.matmul(score[k][:, first:first + width], stack[:, unit_par, j, 0, P * i:P * i + P],
                                            stack[:, unit_par, j, 1, 0:width], start=True, stop=True)
                last.then_inc(scored, 1)

            def flip_piece(h, slot, k):
                if k == 0:
                    pe.wait_ge(exp_done, h + 1)
                wait(pe, pt_done, h * 3 + (1 if k == 2 else 0))
                lo, hi = PIECE_AT[k]
                for col in range(lo, hi, P):
                    last = nc.tensor.transpose(flip[k][:, col - lo:col - lo + P], probs[:, slot, col:col + P], ident)
                last.then_inc(flipped, 1)

            def step(s, par, batch):
                done = 0
                for j in range(HG):
                    scores, flips = has(s, -1), has(s, -1 if j else -2)
                    h = (s - 1) * HG + j

                    def project_next(count):
                        nonlocal done
                        if has(s, 0):
                            project(s, par, batch, range(done, done + count))
                            done += count

                    if isinstance(s, int) and s == 1 and j == 0:
                        project_next(12)
                    if scores:
                        pe.wait_ge(stacked[j], s * 64)
                        score_piece(h, j, 1 - par, 0)
                        score_piece(h, j, 1 - par, 1)
                    if not (isinstance(s, int) and s == 1 and j == 0):
                        project_next(6)
                    if j == 3 and has(s, -2):
                        pe.wait_ge(att_done, (s - 1) * 2)
                        pe.wait_ge(v_rest_done, min(s, UNITS) if isinstance(s, int) else s)
                        for b in range(TB):
                            last = nc.tensor.transpose(misc[:, P * b:P * b + P],
                                                       att[:, b, :, :].rearrange("p h c -> p (h c)"), ident)
                        last.then_inc(att_flipped, 1)
                    if flips:
                        flip_piece(h - 1, (j - 1) % 2, 0)
                        flip_piece(h - 1, (j - 1) % 2, 1)
                    if not (isinstance(s, int) and s == 1 and j == 0):
                        project_next(3)
                    if j == 0 and has(s, -1):
                        pe.wait_ge(v_t_done, s)
                        wait(pe, att_t_done, s - 2)
                        for b in range(TB):
                            last = nc.tensor.transpose(misc[:, P * b:P * b + P], v_t[:, P * b:P * b + P], ident)
                        last.then_inc(v_flipped, 1)
                    if scores:
                        score_piece(h, j, 1 - par, 2)
                    if not (isinstance(s, int) and s == 1 and j == 0):
                        project_next(3)
                    if flips:
                        flip_piece(h - 1, (j - 1) % 2, 2)
                    project_next(6)
                    if has(s, -1 if j >= 2 else -2):
                        head, unit_par = (j - 2) % HG, 1 - par if j >= 2 else par
                        pe.wait_ge(pt_done, (h - 2) * 3 + 3)
                        if head == 0:
                            pe.wait_ge(v_done, s)
                        wait(pe, o_sum_done, h - 2)
                        for i in range(TB):
                            for n in range(2 * (i + 1)):
                                key, half = n // 2, n % 2
                                col, first = BLOCK_AT[i] + P * key, i * VP * HD
                                last = nc.tensor.matmul(
                                    o_ps[:, first:first + VP * HD], pt_half[half][:, head % 2, col:col + P],
                                    v[:, unit_par, key, head, :, :].rearrange("p x c -> p (x c)"),
                                    start=(n == 0), stop=(n == 2 * i + 1))
                        last.then_inc(o_done, 1)

            steps(pe, step)


def layernorm_stats(nc, dve, x, first, stats, block, done):
    for half in range(HALVES):
        last = nc.vector.bn_stats(stats[:, block, half, :], x[:, first, BANK * half:BANK * half + BANK])
    last.then_inc(done, 1)


class DenseFetch:

    CHUNKS = 4

    def __init__(self, sem, w_raw, a_raw, resid, dram):
        self.att_stored = sem("att_stored")
        self.resid, self.resid_in = resid, [sem(f"resid_in{b}") for b in range(B)]
        self.w_raw, self.a_raw, self.dram = w_raw, a_raw, dram
        self.w_in = [sem(f"dw_in{k}") for k in range(2)]
        self.a_in = [sem(f"a_in{k}") for k in range(self.CHUNKS)]

    def start(self, sp):
        for slot in range(2):
            sp.dma_start(self.w_raw[:, slot, :, :].rearrange("p c n -> p (c n)"),
                         self.dram["dense"][slot, :, :]).then_inc(self.w_in[slot], 16)
        for n in range(self.CHUNKS):
            sp.dma_start(self.a_raw[:, n, :], self.dram["att_t"][n, :, :]).then_inc(self.a_in[n], 16)
        self.load_resid(sp, 0)

    def load_resid(self, sp, b):
        sp.dma_start(self.resid[:, b * TB:b * TB + TB, :],
                     self.dram["x"][b, :, :, :].rearrange("t p d -> p t d")).then_inc(self.resid_in[b], 16)


class ContextFetch:

    RING = 4

    def __init__(self, sem, ctx_raw, dram):
        self.raw, self.dram = ctx_raw, dram
        self.done = [sem(f"ctx_in{k}") for k in range(self.RING)]

    def start(self, sp):
        for k in range(self.RING):
            sp.dma_start(self.raw[:, k, :], self.dram["ctx"][k, :, :]).then_inc(self.done[k], 16)


class GateUpFetch:

    def __init__(self, sem, gu, dram):
        self.gu, self.dram = gu, dram
        self.done = [sem(f"gu_in{k}") for k in range(2)]

    def start(self, sp, slot):
        sp.dma_start(self.gu[:, slot, :, :, :].rearrange("p g c n -> p (g c n)"),
                     self.dram["gate_up"][slot, :, :]).then_inc(self.done[slot], 16)


def dense(nc, sem, place, at, fetch, context_fetch, consts, out_bias, query_bias, key_bias, resid, t0_half, t1_half,
          shift, dram):
    fp32, fp32r = mybir.dt.float32, mybir.dt.float32r
    ALU, ACT = mybir.AluOpType, mybir.ActivationFunctionType
    OUT, QUERY, KEY = range(3)
    AR = DenseFetch.CHUNKS
    BLOCKS = 3 * B * C

    def sb(name, shape, dtype):
        nonlocal at
        t, at = place(name, shape, dtype, at)
        return t

    w_half = [sb("dw_hi", [P, 2, C, P], fp32r), sb("dw_lo", [P, 2, C, P], fp32r)]
    w_raw, a_raw = fetch.w_raw, fetch.a_raw
    y_t = sb("y_t", [P, 2, T], fp32)
    part = sb("part", [P, T], fp32)
    dot = sb("dot", [P, B, T], fp32)
    ones = sb("ones", [P, 2], fp32)
    stats = sb("stats", [P, TB, HALVES, 6], fp32)
    mean_var = sb("mean_var", [P, TB, 2], fp32)
    std = sb("std", [P, TB], fp32)
    eps = sb("eps", [P, 1], fp32)
    inv_std = sb("inv_std", [P, TB], fp32)
    ident = consts[:, IDENT:IDENT + P]

    vectors_in = sem("vectors_in")
    resid_in = fetch.resid_in
    a_in, w_in = fetch.a_in, fetch.w_in
    a_hi_done = sem("a_hi_done")
    a_done = sem("a_done")
    w_hi_done = sem("dw_hi_done")
    w_done = sem("dw_done")
    block_done = sem("block_done")
    y_done = sem("y_done")
    y_flipped = sem("y_flipped")
    y_added = sem("y_added")
    dot_zero = sem("dot_zero")
    ones_done = sem("ones_done")
    stats_done = sem("stats_done")
    aggr_done = sem("aggr_done")
    std_done = sem("std_done")
    inv_done = sem("inv_std_done")
    x1_done = sem("x1_done")
    x1_flipped = sem("x1_flipped")
    x1_hi_done = sem("x1_hi_done")
    x1_t_done = sem("x1_t_done")
    out_hi_done = sem("out_hi_done")
    out_done = sem("out_done")
    part_done = sem("part_done")
    dot_done = sem("dot_done")
    shift_ps_done = sem("shift_ps_done")
    shift_done = sem("shift_done")

    with ExitStack() as scope:
        def bank(name):
            return scope.enter_context(nc.psum_tensor(name, [P, BANK], fp32))

        acc = [bank("acc0"), bank("acc1")]
        y_ps = bank("y_ps")
        x1_ps = [bank("x1_ps0"), bank("x1_ps1")]
        shift_ps = [y_ps, bank("shift_ps")]
        block = scope.enter_context(nc.Block())

        def resid_cols(n):
            return bass.ds(n * P, P) if not isinstance(n, int) else slice(n * P, n * P + P)

        def at_block(n):
            return bass.ds(n, 1) if not isinstance(n, int) else slice(n, n + 1)

        @block.sync
        def _(sp):
            def load_w(w, slot, source):
                wait(sp, w_done, w - 1)
                sp.dma_start(w_raw[:, slot, :, :].rearrange("p c n -> p (c n)"),
                             dram["dense"][at_block(source), :, :].rearrange("a p n -> p (a n)")).then_inc(w_in[slot], 16)

            def load_a(n):
                wait(sp, a_done, n - AR + 1)
                sp.dma_start(a_raw[:, n % AR, :], dram["att_t"][n, :, :]).then_inc(a_in[n % AR], 16)

            for n in range(AR, C):
                load_a(n)
            for target, name in ((out_bias, "out_bias"), (query_bias, "query_bias"), (key_bias, "key_bias")):
                sp.dma_start(target[:, :], dram[name]).then_inc(vectors_in, 16)
            load_w(2, 0, 2)
            load_w(3, 1, 3)
            sp.wait_ge(fetch.att_stored, 16 * UNITS)
            for n in range(C, C + AR):
                load_a(n)
            fetch.load_resid(sp, 1)
            for n in range(C // 2, C):
                load_w(n, n % 2, n)
                load_a(C + n)
            for q in range(1, 3 * B):
                with sp.Fori(0, C // 2) as i:
                    for p in range(2):
                        load_w(i * 2 + (q * C + p), p, i * 2 + (q // B * C + p))
            sp.wait_ge(a_done, B * C)
            context_fetch.start(sp)

        @block.gpsimd
        def _(pool):
            def split_w(w, p):
                pool.wait_ge(w_hi_done, w + 1)
                nc.gpsimd.tensor_tensor(w_half[LO][:, p, :, :], w_raw[:, p, :, :],
                                        w_half[HI][:, p, :, :].bitcast(fp32), ALU.subtract).then_inc(w_done, 1)

            split_w(1, 1)
            with pool.Fori(1, BLOCKS // 2) as i:
                for p in range(2):
                    split_w(i * 2 + p, p)

        @block.scalar
        def _(act):
            def split_a(n):
                act.wait_ge(a_in[n % AR], n // AR * 16 + 16)
                nc.scalar.activation(t0_half[HI][:, n // C, n % C, :], a_raw[:, n % AR, :], ACT.Copy).then_inc(a_hi_done, 1)

            def split_w(w, slot, turn):
                act.wait_ge(w_in[slot], turn * 16 + 16)
                wait(act, block_done, w - 1)
                nc.scalar.activation(w_half[HI][:, slot, :, :], w_raw[:, slot, :, :], ACT.Copy).then_inc(w_hi_done, 1)

            def block_out(q, n, p):
                kind, b, w = q // B, q % B, n + q * C
                act.wait_ge(block_done, w + 1)
                if kind == OUT:
                    wait(act, y_flipped, w - 1)
                    act.wait_ge(vectors_in, 48)
                    nc.scalar.activation(y_t[:, p, :], acc[p][:, :], ACT.Identity,
                                         bias=out_bias[:, at_block(n)]).then_inc(y_done, 1)
                else:
                    act.wait_ge(vectors_in, 48)
                    to = (t0_half if kind == QUERY else t1_half)[HI][:, b, at_block(n), :].rearrange("p a t -> p (a t)")
                    if kind == QUERY:
                        nc.scalar.activation(to, acc[p][:, :], ACT.Identity,
                                             bias=query_bias[:, at_block(n)]).then_inc(out_hi_done, 1)
                    else:
                        nc.scalar.activation(to, acc[p][:, :], ACT.Copy).then_inc(out_hi_done, 1)

            def x1_hi(b, c):
                act.wait_ge(x1_flipped, b * C + c + 1)
                nc.scalar.activation(t1_half[HI][:, b, c, :], x1_ps[c % 2][:, :], ACT.Copy).then_inc(x1_hi_done, 1)

            split_w(0, 0, 0)
            for n in range(AR):
                split_a(n)
            split_w(1, 1, 0)
            for n in range(AR, C):
                split_a(n)
            for q in range(3 * B):
                if q == 0:
                    for n in range(C):
                        split_a(C + n)
                        block_out(q, n, n % 2)
                        split_w(n + 2, n % 2, n // 2 + 1)
                elif q > B:
                    count = C // 2 - (q == 3 * B - 1)
                    with act.Fori(0, count) as i:
                        for p in range(2):
                            n = i * 2 + p
                            block_out(q, n, p)
                            split_w(n + (q * C + 2), p, i + (q * C // 2 + 1))
                    if count < C // 2:
                        block_out(q, C - 2, 0)
                        block_out(q, C - 1, 1)
                else:
                    normed = q - 1
                    for n in range(C):
                        block_out(q, n, n % 2)
                        split_w(q * C + n + 2, n % 2, (q * C + n) // 2 + 1)
                        if n == 1:
                            act.wait_ge(ones_done, 1)
                            act.wait_ge(aggr_done, (normed + 1) * TB)
                            nc.scalar.activation(std[:, :], mean_var[:, :, 1], ACT.Sqrt, bias=eps[:, :]).then_inc(std_done, 1)
                        if n >= 4:
                            x1_hi(normed, (n - 4) * 2)
                            x1_hi(normed, (n - 4) * 2 + 1)
            act.wait_ge(ones_done, 1)
            nc.scalar.activation(std[:, 0:1], eps[:, :], ACT.Exp, bias=0.0)

        @block.vector
        def _(dve):
            def split_a(n):
                dve.wait_ge(a_hi_done, n + 1)
                nc.vector.tensor_tensor(t0_half[LO][:, n // C, n % C, :], a_raw[:, n % AR, :],
                                        t0_half[HI][:, n // C, n % C, :].bitcast(fp32), ALU.subtract).then_inc(a_done, 1)

            def add_y(b, n, w):
                dve.wait_ge(y_flipped, w + 1)
                dve.wait_ge(resid_in[b], 16)
                cols = resid[:, b * TB:b * TB + TB, resid_cols(n)]
                nc.vector.tensor_tensor(cols, y_ps[:, :].rearrange("p (t c) -> p t c", t=TB), cols, ALU.add).then_inc(y_added, 1)

            def block_lo(q, n, p):
                kind, b = q // B, q % B
                half = t0_half if kind == QUERY else t1_half
                hi = half[HI][:, b, at_block(n), :].rearrange("p a t -> p (a t)").bitcast(fp32)
                lo = half[LO][:, b, at_block(n), :].rearrange("p a t -> p (a t)")
                dve.wait_ge(out_hi_done, n + ((q - B) * C + 1))
                if kind == KEY:
                    nc.vector.tensor_tensor(lo, acc[p][:, :], hi, ALU.subtract).then_inc(out_done, 1)
                    return
                wait(dve, dot_done, n + (q - B) * C)
                nc.vector.tensor_scalar(part[:, :], acc[p][:, :], query_bias[:, at_block(n)], key_bias[:, at_block(n)],
                                        ALU.add, ALU.mult).then_inc(part_done, 1)
                nc.vector.scalar_tensor_tensor(out=lo, in0=acc[p][:, :], scalar=query_bias[:, at_block(n)], in1=hi,
                                               op0=ALU.add, op1=ALU.subtract).then_inc(out_done, 1)
                dve.wait_ge(part_done, n + ((q - B) * C + 1))
                nc.vector.tensor_tensor(dot[:, b, :], dot[:, b, :], part[:, :], ALU.add).then_inc(dot_done, 1)

            def x1_lo(b, c):
                dve.wait_ge(x1_hi_done, b * C + c + 1)
                nc.vector.tensor_tensor(t1_half[LO][:, b, c, :], x1_ps[c % 2][:, :],
                                        t1_half[HI][:, b, c, :].bitcast(fp32), ALU.subtract).then_inc(x1_t_done, 1)

            def norm_part(b, n):
                if n < 2:
                    for t in (2 * n, 2 * n + 1):
                        dve.wait_ge(y_added, (b + 1) * C)
                        if b:
                            dve.wait_ge(x1_done, b * TB)
                        layernorm_stats(nc, dve, resid, b * TB + t, stats, t, stats_done)
                        dve.wait_ge(stats_done, b * TB + t + 1)
                        nc.vector.bn_aggr(mean_var[:, t, :], stats[:, t, :, :].rearrange("p h s -> p (h s)")).then_inc(aggr_done, 1)
                elif n == 2:
                    dve.wait_ge(std_done, b + 1)
                    nc.vector.reciprocal(inv_std[:, :], std[:, :]).then_inc(inv_done, 1)
                    dve.wait_ge(inv_done, b + 1)
                if n in (2, 3):
                    for t in (2 * n - 4, 2 * n - 3):
                        rows = resid[:, b * TB + t, :]
                        nc.vector.tensor_scalar(rows, rows, mean_var[:, t, 0:1], inv_std[:, t:t + 1],
                                                ALU.subtract, ALU.mult).then_inc(x1_done, 1)

            dve.wait_ge(w_hi_done, 1)
            nc.vector.tensor_tensor(w_half[LO][:, 0, :, :], w_raw[:, 0, :, :],
                                    w_half[HI][:, 0, :, :].bitcast(fp32), ALU.subtract).then_inc(w_done, 1)
            for n in range(C):
                split_a(n)
            dve.wait_ge(fetch.att_stored, 16 * UNITS)
            nc.vector.memset(eps[:, :], EPS)
            nc.vector.memset(dot[:, :, :], 0.0).then_inc(dot_zero, 1)
            nc.vector.memset(ones[:, :], 1.0).then_inc(ones_done, 1)
            for n in range(C):
                split_a(C + n)
                add_y(0, n, n)
            for n in range(C):
                norm_part(0, n)
                if n >= 4:
                    x1_lo(0, (n - 4) * 2)
                    x1_lo(0, (n - 4) * 2 + 1)
                add_y(1, n, C + n)
            dve.wait_ge(vectors_in, 48)
            dve.wait_ge(dot_zero, 1)
            for n in range(C):
                norm_part(1, n)
                block_lo(B, n, n % 2)
                if n >= 4:
                    x1_lo(1, (n - 4) * 2)
                    x1_lo(1, (n - 4) * 2 + 1)
            for q in range(B + 1, 3 * B):
                with dve.Fori(0, C // 2) as i:
                    for p in range(2):
                        block_lo(q, i * 2 + p, p)
            for b in range(B):
                dve.wait_ge(shift_ps_done, b + 1)
                nc.vector.tensor_copy(shift[:, b * TB:b * TB + TB], shift_ps[b][:, 0:TB]).then_inc(shift_done, 1)
            dve.wait_ge(shift_done, B)

        @block.tensor
        def _(pe):
            def half_block(q, n, p, part):
                kind, b, w = q // B, q % B, n + q * C
                moving = t1_half if kind == QUERY else t0_half
                if part == 0:
                    pe.wait_ge(w_done, w + 1)
                    if kind == OUT:
                        wait(pe, y_done, w - 1)
                    elif isinstance(n, int) and n < 2 and q <= B:
                        wait(pe, y_done, w - 1)
                    else:
                        wait(pe, out_done, w - (B * C + 1))
                for c in range(part * C // 2, (part + 1) * C // 2):
                    if q == 0 and isinstance(n, int) and n == 0:
                        pe.wait_ge(a_done, c + 1)
                    if kind == QUERY and isinstance(n, int) and n == 0:
                        pe.wait_ge(x1_t_done, b * C + c + 1)
                    for k, (s, m) in enumerate(PAIRS):
                        last = nc.tensor.matmul(acc[p][:, :], w_half[s][:, p, c, :], moving[m][:, b, c, :],
                                                start=(c == 0 and k == 0), stop=(c == C - 1 and k == 2))
                if part == 1:
                    last.then_inc(block_done, 1)

            def flip_y(w, p):
                pe.wait_ge(y_done, w + 1)
                wait(pe, y_added, w)
                for t in range(TB):
                    last = nc.tensor.transpose(y_ps[:, P * t:P * t + P], y_t[:, p, P * t:P * t + P], ident)
                last.then_inc(y_flipped, 1)

            def flip_x1(b, c):
                if c == 0:
                    pe.wait_ge(x1_done, (b + 1) * TB)
                wait(pe, x1_t_done, b * C + c - 1)
                for t in range(TB):
                    last = nc.tensor.transpose(x1_ps[c % 2][:, P * t:P * t + P],
                                               resid[:, b * TB + t, P * c:P * c + P], ident)
                last.then_inc(x1_flipped, 1)

            def sum_dot(b):
                pe.wait_ge(dot_done, (b + 1) * C)
                for t in range(TB):
                    last = nc.tensor.matmul(shift_ps[b][:, t:t + 1], dot[:, b, P * t:P * t + P],
                                            ones[:, 0:1], start=True, stop=True)
                last.then_inc(shift_ps_done, 1)

            def one_block(q, n, p, flips):
                half_block(q, n, p, 0)
                if flips:
                    flip_y(n + (q * C - 1), 1 - p)
                half_block(q, n, p, 1)

            one_block(0, 0, 0, False)
            one_block(0, 1, 1, True)
            with pe.Fori(1, C // 2) as i:
                for p in range(2):
                    one_block(0, i * 2 + p, p, True)
            pe.wait_ge(a_done, B * C)
            with pe.Fori(0, C // 4) as i:
                for p in range(2):
                    one_block(1, i * 2 + p, p, True)
            for n in range(C // 2, C):
                one_block(1, n, n % 2, True)
                flip_x1(0, 2 * (n - 4))
                flip_x1(0, 2 * (n - 4) + 1)
            for n in range(C):
                one_block(2, n, n % 2, n == 0)
                if n >= 4:
                    flip_x1(1, 2 * (n - 4))
                    flip_x1(1, 2 * (n - 4) + 1)
            one_block(3, 0, 0, False)
            one_block(3, 1, 1, False)
            with pe.Fori(1, C // 2) as i:
                for p in range(2):
                    one_block(3, i * 2 + p, p, False)
            for q in (4, 5):
                pe.wait_ge(out_done, (q - 3) * C)
                with pe.Fori(0, C // 2) as i:
                    for p in range(2):
                        one_block(q, i * 2 + p, p, False)
                if q == 4:
                    sum_dot(0)
            sum_dot(1)


def cross(nc, sem, place, at, fetch, gate_up_fetch, x2t_half, consts, resid, t1_half, shift, dram):
    fp32, fp32r = mybir.dt.float32, mybir.dt.float32r
    ALU, ACT = mybir.AluOpType, mybir.ActivationFunctionType
    scale = float(D) ** -0.5
    RING = ContextFetch.RING
    PHASES = 4 * B
    CHUNKS = PHASES * C
    SCORES = 2 * B

    def sb(name, shape, dtype):
        nonlocal at
        t, at = place(name, shape, dtype, at)
        return t

    sx = sb("sx", [P, B, TB, D], fp32)
    ctx_raw = fetch.raw
    ctx_half = [sb("ctx_hi", [P, RING, BANK], fp32r), sb("ctx_lo", [P, RING, BANK], fp32r)]
    top = sb("c_top", [P, B, TB], fp32)
    top_shift = sb("top_shift", [P, B, TB], fp32)
    exp_bias = sb("exp_bias", [P, B, TB], fp32)
    sums = sb("c_sums", [P, B, TB], fp32)
    inv_sums = sb("c_inv_sums", [P, B, TB], fp32)
    stats = sb("c_stats", [P, TB, HALVES, 6], fp32)
    mean_var = sb("c_mean_var", [P, TB, 2], fp32)
    std = sb("c_std", [P, TB], fp32)
    inv_std = sb("c_inv_std", [P, TB], fp32)
    eps = sb("c_eps", [P, 1], fp32)
    warm = sb("c_warm", [P, 1], fp32)
    ident = consts[:, IDENT:IDENT + P]

    ctx_in = fetch.done
    ctx_hi_done = sem("ctx_hi_done")
    ctx_done = sem("ctx_done")
    ctx_used = sem("ctx_used")
    acc_done = sem("acc_done")
    s_out = sem("s_out")
    top_done = sem("c_top_done")
    top_shift_done = sem("top_shift_done")
    bias_done = sem("exp_bias_done")
    exp_done = sem("c_exp_done")
    inv_sums_done = sem("inv_sums_done")
    p_flipped = sem("p_flipped")
    p_hi_done = sem("p_hi_done")
    p_done = sem("p_done")
    av_out = sem("av_out")
    eps_done = sem("c_eps_done")
    stats_done = sem("c_stats_done")
    aggr_done = sem("c_aggr_done")
    std_done = sem("c_std_done")
    inv_done = sem("c_inv_done")
    x2_done = sem("x2_done")
    x2_flipped = sem("x2_flipped")
    x2_hi_done = sem("x2_hi_done")
    x2_t_done = sem("x2_t_done")

    with ExitStack() as scope:
        banks = [scope.enter_context(nc.psum_tensor(f"c_bank{k}", [P, BANK], fp32)) for k in range(8)]
        block = scope.enter_context(nc.Block())

        def bank_done(engine, phase, t):
            if t < TB - 1:
                engine.wait_ge(acc_done, phase * (TB - 1) + t + 1)
            else:
                engine.wait_ge(ctx_used, (phase + 1) * C)

        @block.sync
        def _(sp):
            def load(k, slot):
                wait(sp, ctx_done, k - RING + 1)
                sp.dma_start(ctx_raw[:, slot, :], dram["ctx"][bass.ds(k, 1), :, :].rearrange("a p n -> p (a n)")
                             ).then_inc(ctx_in[slot], 16)

            with sp.Fori(1, CHUNKS // RING) as i:
                for slot in range(RING):
                    load(i * RING + slot, slot)
            for slot in range(2):
                sp.wait_ge(ctx_done, CHUNKS - RING // 2 * (1 - slot))
                gate_up_fetch.start(sp, slot)

        @block.scalar
        def _(act):
            def split(k):
                act.wait_ge(ctx_in[k % RING], k // RING * 16 + 16)
                wait(act, ctx_used, k - RING + 1)
                nc.scalar.activation(ctx_half[HI][:, k % RING, :], ctx_raw[:, k % RING, :], ACT.Copy).then_inc(ctx_hi_done, 1)

            def after(phase, c):
                if c == C - 1 and phase < SCORES:
                    b, half = phase // 2, phase % 2
                    for t in range(TB):
                        bank_done(act, phase, t)
                        nc.scalar.activation(sx[:, b, t, BANK * half:BANK * half + BANK], banks[phase % 2 * TB + t][:, :],
                                             ACT.Copy).then_inc(s_out, 1)
                if phase in (2, 4) and c >= 4:
                    b, t = phase // 2 - 1, c - 4
                    act.wait_ge(bias_done, b + 1)
                    nc.scalar.activation(sx[:, b, t, :], sx[:, b, t, :], ACT.Exp, bias=exp_bias[:, b, t:t + 1],
                                         scale=scale, accum_out=sums[:, b, t:t + 1]).then_inc(exp_done, 1)
                if phase in (3, 5) and 1 <= c <= 4:
                    b = phase // 2 - 1
                    for n in (2 * c - 2, 2 * c - 1):
                        act.wait_ge(p_flipped, b * C + n + 1)
                        nc.scalar.activation(t1_half[HI][:, b, n, :], banks[n % 2][:, :], ACT.Copy).then_inc(p_hi_done, 1)
                if phase == 6 and c == 2:
                    act.wait_ge(aggr_done, TB)
                    nc.scalar.activation(std[:, :], mean_var[:, :, 1], ACT.Sqrt, bias=eps[:, :]).then_inc(std_done, 1)
                if phase == 7 and 1 <= c <= 4:
                    for n in (2 * c - 2, 2 * c - 1):
                        act.wait_ge(x2_flipped, n + 1)
                        nc.scalar.activation(x2t_half[HI][:, 0, n, :], banks[n % 2][:, :], ACT.Copy,
                                             scale=FP16_UP).then_inc(x2_hi_done, 1)

            act.wait_ge(eps_done, 1)
            for k in range(RING):
                split(k)
            for k in range(CHUNKS):
                if k + RING < CHUNKS:
                    split(k + RING)
                after(k // C, k % C)
            nc.scalar.activation(warm[:, :], eps[:, :], ACT.Silu)

        @block.vector
        def _(dve):
            def split(k):
                dve.wait_ge(ctx_hi_done, k + 1)
                nc.vector.tensor_tensor(ctx_half[LO][:, k % RING, :], ctx_raw[:, k % RING, :],
                                        ctx_half[HI][:, k % RING, :].bitcast(fp32), ALU.subtract).then_inc(ctx_done, 1)

            def after(phase, c):
                if phase in (2, 4) and c < TB:
                    b = phase // 2 - 1
                    dve.wait_ge(s_out, (phase - 1) * TB + c + 1)
                    nc.vector.tensor_reduce(top[:, b, c:c + 1], sx[:, b, c, :], mybir.AxisListType.X,
                                            ALU.max).then_inc(top_done, 1)
                if phase in (2, 4) and c == TB - 1:
                    b = phase // 2 - 1
                    rows = shift[:, b * TB:b * TB + TB]
                    dve.wait_ge(top_done, (b + 1) * TB)
                    nc.vector.tensor_tensor(top_shift[:, b, :], top[:, b, :], rows, ALU.add).then_inc(top_shift_done, 1)
                    dve.wait_ge(top_shift_done, 2 * b + 1)
                    nc.vector.tensor_tensor(top_shift[:, b, :], rows, top_shift[:, b, :], ALU.subtract).then_inc(top_shift_done, 1)
                    dve.wait_ge(top_shift_done, 2 * b + 2)
                    nc.vector.tensor_scalar(exp_bias[:, b, :], top_shift[:, b, :], scale, None, ALU.mult).then_inc(bias_done, 1)
                if phase in (3, 5) and c == 0:
                    b = phase // 2 - 1
                    dve.wait_ge(exp_done, (b + 1) * TB)
                    nc.vector.reciprocal(inv_sums[:, b, :], sums[:, b, :]).then_inc(inv_sums_done, 1)
                if phase in (3, 5) and 1 <= c <= 4:
                    b = phase // 2 - 1
                    for n in (2 * c - 2, 2 * c - 1):
                        dve.wait_ge(p_hi_done, b * C + n + 1)
                        nc.vector.tensor_tensor(t1_half[LO][:, b, n, :], banks[n % 2][:, :],
                                                t1_half[HI][:, b, n, :].bitcast(fp32), ALU.subtract).then_inc(p_done, 1)
                if c == C - 1 and phase >= SCORES:
                    b, half = (phase - SCORES) // 2, phase % 2
                    dve.wait_ge(inv_sums_done, b + 1)
                    for t in range(TB):
                        bank_done(dve, phase, t)
                        cols = resid[:, b * TB + t, BANK * half:BANK * half + BANK]
                        nc.vector.scalar_tensor_tensor(out=cols, in0=banks[phase % 2 * TB + t][:, :],
                                                       scalar=inv_sums[:, b, t:t + 1], in1=cols,
                                                       op0=ALU.mult, op1=ALU.add).then_inc(av_out, 1)
                if phase == 6 and c < 2:
                    for t in (2 * c, 2 * c + 1):
                        dve.wait_ge(av_out, 2 * TB)
                        layernorm_stats(nc, dve, resid, t, stats, t, stats_done)
                        dve.wait_ge(stats_done, t + 1)
                        nc.vector.bn_aggr(mean_var[:, t, :], stats[:, t, :, :].rearrange("p h s -> p (h s)")).then_inc(aggr_done, 1)
                if phase == 6 and c == 3:
                    dve.wait_ge(std_done, 1)
                    nc.vector.reciprocal(inv_std[:, :], std[:, :]).then_inc(inv_done, 1)
                    dve.wait_ge(inv_done, 1)
                if phase == 6 and c in (3, 4):
                    for t in (2 * c - 6, 2 * c - 5):
                        nc.vector.tensor_scalar(resid[:, t, :], resid[:, t, :], mean_var[:, t, 0:1], inv_std[:, t:t + 1],
                                                ALU.subtract, ALU.mult).then_inc(x2_done, 1)
                if phase == 7 and 1 <= c <= 4:
                    for n in (2 * c - 2, 2 * c - 1):
                        dve.wait_ge(x2_hi_done, n + 1)
                        nc.vector.scalar_tensor_tensor(out=x2t_half[LO][:, 0, n, :], in0=banks[n % 2][:, :], scalar=FP16_UP,
                                                       in1=x2t_half[HI][:, 0, n, :], op0=ALU.mult,
                                                       op1=ALU.subtract).then_inc(x2_t_done, 1)

            nc.vector.memset(eps[:, :], EPS).then_inc(eps_done, 1)
            for k in range(RING):
                split(k)
            for k in range(CHUNKS):
                if k + RING < CHUNKS:
                    split(k + RING)
                after(k // C, k % C)

        @block.tensor
        def _(pe):
            for phase in range(PHASES):
                attends = phase >= SCORES
                b = (phase - SCORES) // 2 if attends else phase // 2
                if phase in (2, 3):
                    pe.wait_ge(s_out, (phase - 1) * TB)
                elif phase == 4:
                    pe.wait_ge(p_done, C)
                elif phase == 5:
                    pe.wait_ge(s_out, SCORES * TB)
                elif phase == 6:
                    pe.wait_ge(p_done, 2 * C)
                elif phase == 7:
                    pe.wait_ge(av_out, 2 * TB)
                for c in range(C):
                    k = phase * C + c
                    pe.wait_ge(ctx_done, k + 1)
                    for t in range(TB):
                        for n, (s, m) in enumerate(PAIRS):
                            last = nc.tensor.matmul(banks[phase % 2 * TB + t][:, :], t1_half[s][:, b, c, P * t:P * t + P],
                                                    ctx_half[m][:, k % RING, :], start=(c == 0 and n == 0),
                                                    stop=(c == C - 1 and n == 2))
                        if c == C - 1 and t < TB - 1:
                            last.then_inc(acc_done, 1)
                    last.then_inc(ctx_used, 1)
                    if phase in (3, 5) and 1 <= c <= 4:
                        pb = phase // 2 - 1
                        if c == 1:
                            if pb == 0:
                                pe.wait_ge(s_out, 3 * TB)
                            else:
                                pe.wait_ge(av_out, TB)
                            pe.wait_ge(exp_done, (pb + 1) * TB)
                        for n in (2 * c - 2, 2 * c - 1):
                            wait(pe, p_done, pb * C + n - 1)
                            for t in range(TB):
                                last = nc.tensor.transpose(banks[n % 2][:, P * t:P * t + P], sx[:, pb, t, P * n:P * n + P], ident)
                            last.then_inc(p_flipped, 1)
                    if phase == 7 and 1 <= c <= 4:
                        if c == 1:
                            pe.wait_ge(av_out, 3 * TB)
                            pe.wait_ge(x2_done, TB)
                        for n in (2 * c - 2, 2 * c - 1):
                            wait(pe, x2_t_done, n - 1)
                            for t in range(TB):
                                last = nc.tensor.transpose(banks[n % 2][:, P * t:P * t + P], resid[:, t, P * n:P * n + P], ident)
                            last.then_inc(x2_flipped, 1)


def ffn(nc, sem, place, at, top, x2t_at, fetch, x2t_half, consts, resid, dram):
    fp32, fp32r, fp16 = mybir.dt.float32, mybir.dt.float32r, mybir.dt.float16
    ALU, ACT = mybir.AluOpType, mybir.ActivationFunctionType
    PEELED = 8
    DOWN = HALVES * MB
    WD = 4
    LAST = 8
    DOWN_UP = 1.0 / FP16_UP

    def sb(name, shape, dtype):
        nonlocal at
        t, at = place(name, shape, dtype, at)
        return t

    h_half = [sb("h_hi", [P, MB, T], fp32r), sb("h_lo", [P, MB, T], fp32r)]
    wd_last, _ = place("wd_last", [P, LAST, BANK], fp32r, x2t_at)
    gu = fetch.gu
    wd = sb("wd", [P, WD, BANK], fp32r)
    wd_raw = sb("wd_raw", [P, 2, 2, BANK], fp16)
    gated = sb("gated", [P, 2, T], fp32)
    at = top
    stats = sb("f_stats", [P, TB, HALVES, 6], fp32)
    mean_var = sb("f_mean_var", [P, TB, 2], fp32)
    std = sb("f_std", [P, TB], fp32)
    inv_std = sb("f_inv_std", [P, TB], fp32)
    eps = sb("f_eps", [P, 1], fp32)
    ident = consts[:, IDENT:IDENT + P]

    gu_in = fetch.done
    wd_in = [sem(f"wd_in{k}") for k in range(2)]
    gate_done = sem("gate_done")
    up_done = sem("up_done")
    silu_done = sem("silu_done")
    gated_done = sem("gated_done")
    h_hi_done = sem("h_hi_done")
    h_done = sem("h_done")
    wd_done = sem("wd_done")
    wd_used = sem("wd_used")
    down_done = sem("down_done")
    down_out = sem("down_out")
    last_done = sem("last_done")
    eps_done = sem("f_eps_done")
    first_stats_done = sem("first_stats_done")
    stats_done = sem("f_stats_done")
    aggr_done = sem("f_aggr_done")
    std_done = sem("f_std_done")
    inv_done = sem("f_inv_done")
    norm_done = sem("norm_done")
    x2_flipped = sem("f_x2_flipped")
    x2_hi_done = sem("f_x2_hi_done")
    x2_t_done = sem("f_x2_t_done")
    stored = sem("stored")

    def at_block(n):
        return slice(n, n + 1) if isinstance(n, int) else bass.ds(n, 1)

    with ExitStack() as scope:
        banks = [scope.enter_context(nc.psum_tensor(f"f_bank{k}", [P, BANK], fp32)) for k in range(8)]
        block = scope.enter_context(nc.Block())

        def gate_bank(b, p):
            return banks[4 * b + 2 * p]

        def up_bank(b, p):
            return banks[4 * b + 2 * p + 1]

        def down_bank(b, half, t):
            return banks[4 * ((b + half + 1) % 2) + t]

        @block.sync
        def _(sp):
            def load_gu(b, m, p, turn):
                wait(sp, up_done, b * MB + m - 1)
                sp.dma_start(gu[:, p, :, :, :].rearrange("p g c n -> p (g c n)"),
                             dram["gate_up"][at_block(m), :, :].rearrange("a p n -> p (a n)")).then_inc(gu_in[p], 16)

            def load_wd(b, pair, p):
                wait(sp, wd_done, b * DOWN + pair * 2 - 2)
                sp.dma_start(wd_raw[:, p, :, :].rearrange("p k n -> p (k n)"),
                             dram["down"][at_block(pair), :, :].rearrange("a p n -> p (a n)")).then_inc(wd_in[p], 16)

            def store(b):
                for t in range(TB):
                    sp.wait_ge(norm_done, (b + 1) * TB + t + 1)
                    sp.dma_start(dram["out"][b, t, :, :], resid[:, b * TB + t, :]).then_inc(stored, 16)

            for b in range(B):
                for m in range(0 if b else 2, PEELED):
                    load_gu(b, m, m % 2, 0)
                load_wd(b, 0, 0)
                load_wd(b, 1, 1)
                if b == 1:
                    store(0)
                with sp.Fori(PEELED // 2, MB // 2) as i:
                    for p in range(2):
                        load_gu(b, i * 2 + p, p, i)
                with sp.Fori(1, DOWN // 4) as i:
                    for p in range(2):
                        load_wd(b, i * 2 + p, p)
            store(1)
            sp.wait_ge(stored, 16 * B * TB)

        @block.scalar
        def _(act):
            def step(b, m, p):
                act.wait_ge(gate_done, b * MB + m + 1)
                wait(act, h_done, b * MB + m - 1)
                nc.scalar.activation(gated[:, p, :], gate_bank(b, p)[:, :], ACT.Silu, scale=DOWN_UP).then_inc(silu_done, 1)
                act.wait_ge(gated_done, b * MB + m + 1)
                act.wait_ge(eps_done, 1)
                nc.scalar.activation(h_half[HI][:, at_block(m), :].rearrange("p a t -> p (a t)"), gated[:, p, :],
                                     ACT.Copy).then_inc(h_hi_done, 1)

            def convert(b, i, n):
                if n % 2 == 0:
                    act.wait_ge(wd_in[n // 2], i * 16 + (b * DOWN // 4 * 16 + 16))
                wait(act, wd_used, i * WD + (b * DOWN + n - WD + 1))
                nc.scalar.activation(wd[:, n, :], wd_raw[:, n // 2, n % 2, :], ACT.Copy).then_inc(wd_done, 1)

            def square_root(turn):
                act.wait_ge(aggr_done, (turn + 1) * TB)
                nc.scalar.activation(std[:, :], mean_var[:, :, 1], ACT.Sqrt, bias=eps[:, :]).then_inc(std_done, 1)

            act.wait_ge(eps_done, 1)
            for b in range(B):
                for m in range(PEELED):
                    step(b, m, m % 2)
                    if m == 1:
                        square_root(b)
                    if b == 0 and m >= PEELED - C // 2:
                        for c in (2 * m - 2 * PEELED + C, 2 * m - 2 * PEELED + C + 1):
                            act.wait_ge(x2_flipped, c + 1)
                            nc.scalar.activation(x2t_half[HI][:, 1, c, :], banks[4 + c % 2][:, :], ACT.Copy,
                                                 scale=FP16_UP).then_inc(x2_hi_done, 1)
                for n in range(WD):
                    convert(b, 0, n)
                with act.Fori(PEELED // 2, MB // 2) as i:
                    for p in range(2):
                        step(b, i * 2 + p, p)
                with act.Fori(1, (DOWN - (LAST if b == B - 1 else 0)) // WD) as i:
                    for n in range(WD):
                        convert(b, i, n)
            for n in range(LAST):
                pair = (B * DOWN - LAST + n) // 2
                act.wait_ge(wd_in[pair % 2], pair // 2 * 16 + 16)
                nc.scalar.activation(wd_last[:, n, :], wd_raw[:, pair % 2, n % 2, :], ACT.Copy).then_inc(wd_done, 1)
            for t in range(TB):
                act.wait_ge(aggr_done, 2 * TB + t + 1)
                nc.scalar.activation(std[:, t:t + 1], mean_var[:, t, 1:2], ACT.Sqrt, bias=eps[:, :]).then_inc(std_done, 1)

        @block.vector
        def _(dve):
            def step(b, m, p):
                dve.wait_ge(silu_done, b * MB + m + 1)
                dve.wait_ge(up_done, b * MB + m + 1)
                nc.vector.scalar_tensor_tensor(out=gated[:, p, :], in0=up_bank(b, p)[:, :], scalar=DOWN_UP,
                                               in1=gated[:, p, :], op0=ALU.mult, op1=ALU.mult).then_inc(gated_done, 1)
                dve.wait_ge(h_hi_done, b * MB + m + 1)
                nc.vector.tensor_tensor(h_half[LO][:, at_block(m), :].rearrange("p a t -> p (a t)"), gated[:, p, :],
                                        h_half[HI][:, at_block(m), :].rearrange("p a t -> p (a t)").bitcast(fp32),
                                        ALU.subtract).then_inc(h_done, 1)

            def norm_stats(turn, t):
                first = (1, 0, 1)[turn] * TB + t
                wait(dve, down_out, turn * 2 * TB)
                wait(dve, norm_done, turn * TB)
                layernorm_stats(nc, dve, resid, first, stats, t, stats_done)
                dve.wait_ge(stats_done, turn * TB + t + 1)
                nc.vector.bn_aggr(mean_var[:, t, :], stats[:, t, :, :].rearrange("p h s -> p (h s)")).then_inc(aggr_done, 1)

            def inverse(turn):
                dve.wait_ge(std_done, turn + 1)
                nc.vector.reciprocal(inv_std[:, :], std[:, :]).then_inc(inv_done, 1)
                dve.wait_ge(inv_done, turn + 1)

            def normalise(turn, t):
                rows = resid[:, (1, 0, 1)[turn] * TB + t, :]
                nc.vector.tensor_scalar(rows, rows, mean_var[:, t, 0:1], inv_std[:, t:t + 1],
                                        ALU.subtract, ALU.mult).then_inc(norm_done, 1)

            def down(b, half):
                for t in range(TB):
                    turn = b * HALVES + half
                    if t < TB - 1:
                        dve.wait_ge(down_done, turn * (TB - 1) + t + 1)
                    else:
                        dve.wait_ge(wd_used, (turn + 1) * MB)
                    wait(dve, norm_done, (b + 1) * TB if b == 0 else 0)
                    cols = resid[:, b * TB + t, BANK * half:BANK * half + BANK]
                    nc.vector.tensor_tensor(cols, down_bank(b, half, t)[:, :], cols, ALU.add).then_inc(down_out, 1)

            nc.vector.memset(eps[:, :], EPS).then_inc(eps_done, 1)
            for b in range(B):
                for m in range(PEELED):
                    if m < 2:
                        norm_stats(b, 2 * m)
                        norm_stats(b, 2 * m + 1)
                    step(b, m, m % 2)
                    if m == 2:
                        inverse(b)
                    if m in (2, 3):
                        normalise(b, 2 * m - 4)
                        normalise(b, 2 * m - 3)
                    if b == 0 and m >= PEELED - C // 2:
                        for c in (2 * m - 2 * PEELED + C, 2 * m - 2 * PEELED + C + 1):
                            dve.wait_ge(x2_hi_done, c + 1)
                            nc.vector.scalar_tensor_tensor(out=x2t_half[LO][:, 1, c, :], in0=banks[4 + c % 2][:, :],
                                                           scalar=FP16_UP, in1=x2t_half[HI][:, 1, c, :],
                                                           op0=ALU.mult, op1=ALU.subtract).then_inc(x2_t_done, 1)
                with dve.Fori(PEELED // 2, MB // 2) as i:
                    for p in range(2):
                        step(b, i * 2 + p, p)
                down(b, 0)
                if b == 0:
                    down(b, 1)
            dve.wait_ge(down_out, (2 * B - 1) * TB)
            dve.wait_ge(norm_done, 2 * TB)
            for t in range(TB):
                nc.vector.bn_stats(stats[:, t, 0, :], resid[:, TB + t, 0:BANK]).then_inc(first_stats_done, 1)
            for t in range(TB):
                dve.wait_ge(last_done, t + 1)
                cols = resid[:, TB + t, BANK:D]
                nc.vector.tensor_tensor(cols, down_bank(1, 1, t)[:, :], cols, ALU.add).then_inc(down_out, 1)
                dve.wait_ge(down_out, (2 * B - 1) * TB + t + 1)
                nc.vector.bn_stats(stats[:, t, 1, :], cols).then_inc(stats_done, 1)
                dve.wait_ge(first_stats_done, t + 1)
                dve.wait_ge(stats_done, 2 * TB + t + 1)
                nc.vector.bn_aggr(mean_var[:, t, :], stats[:, t, :, :].rearrange("p h s -> p (h s)")).then_inc(aggr_done, 1)
                dve.wait_ge(std_done, 3 + t)
                nc.vector.reciprocal(inv_std[:, t:t + 1], std[:, t:t + 1]).then_inc(inv_done, 1)
                dve.wait_ge(inv_done, 3 + t)
                normalise(2, t)

        @block.tensor
        def _(pe):
            def step(b, m, p, turn):
                pe.wait_ge(gu_in[p], turn * 16 + (b * MB // 2 * 16 + 16))
                for g, (bank, done) in enumerate(((gate_bank(b, p), gate_done), (up_bank(b, p), up_done))):
                    if not (isinstance(m, int) and m < 2):
                        wait(pe, (silu_done, gated_done)[g], b * MB + m - 1)
                    for c in range(C):
                        for half in (HI, LO):
                            last = nc.tensor.matmul(bank[:, :], gu[:, p, g, c, :], x2t_half[half][:, b, c, :],
                                                    start=(c == 0 and half == HI), stop=(c == C - 1 and half == LO))
                    last.then_inc(done, 1)

            def flip_x2(c):
                pe.wait_ge(norm_done, TB)
                wait(pe, x2_t_done, c - 1)
                for t in range(TB):
                    last = nc.tensor.transpose(banks[4 + c % 2][:, P * t:P * t + P],
                                               resid[:, TB + t, P * c:P * c + P], ident)
                last.then_inc(x2_flipped, 1)

            for b in range(B):
                if b == 1:
                    pe.wait_ge(x2_t_done, C)
                    pe.wait_ge(down_out, TB)
                for m in range(PEELED):
                    step(b, m, m % 2, m // 2)
                    if b == 0 and m >= PEELED - C // 2:
                        flip_x2(2 * m - 2 * PEELED + C)
                        flip_x2(2 * m - 2 * PEELED + C + 1)
                with pe.Fori(PEELED // 2, MB // 2) as i:
                    for p in range(2):
                        step(b, i * 2 + p, p, i)
                for half in range(HALVES):
                    if half == 0:
                        if b == 0:
                            pe.wait_ge(x2_t_done, C)
                        else:
                            pe.wait_ge(down_out, 2 * TB)
                    else:
                        pe.wait_ge(gated_done, (b + 1) * MB)
                    straight = LAST if b == B - 1 and half == 1 else 0
                    for m in range(MB - straight):
                        k = half * MB + m
                        pe.wait_ge(wd_done, b * DOWN + k + 1)
                        if half == 0:
                            pe.wait_ge(h_done, b * MB + m + 1)
                        for t in range(TB):
                            for a in (HI, LO):
                                last = nc.tensor.matmul(down_bank(b, half, t)[:, :], h_half[a][:, m, P * t:P * t + P],
                                                        wd[:, k % WD, :], start=(m == 0 and a == HI),
                                                        stop=(m == MB - 1 and a == LO))
                            if m == MB - 1 and t < TB - 1:
                                last.then_inc(down_done, 1)
                        last.then_inc(wd_used, 1)
            pe.wait_ge(wd_done, B * DOWN)
            for t in range(TB):
                for n in range(LAST):
                    for a in (HI, LO):
                        last = nc.tensor.matmul(down_bank(1, 1, t)[:, :], h_half[a][:, MB - LAST + n, P * t:P * t + P],
                                                wd_last[:, n, :], start=False, stop=(n == LAST - 1 and a == LO))
                last.then_inc(last_done, 1)


def decoder_layer(nc, x_t, x, ctx, wqkv, dense_w, gate_up, down, consts_in, qkv_bias_in, out_bias_in,
                  query_bias_in, key_bias_in, att_t, out):
    fp32, fp32r, fp16 = mybir.dt.float32, mybir.dt.float32r, mybir.dt.float16
    FIRST, END = 16512, 229344
    SIZES = {fp32: 4, fp32r: 4, fp16: 2, mybir.dt.bfloat16: 2}

    def place(name, shape, dtype, at):
        size = SIZES[dtype]
        for extent in shape[1:]:
            size *= extent
        after = (at + size + 31) // 32 * 32
        assert after <= END, (name, after)
        return nc.alloc_sbuf_tensor_at(name, shape, dtype, offset=at), after

    consts, at = place("consts", [P, CONSTS], fp32, FIRST)
    qkv_bias, at = place("qkv_bias", [P, 3 * UNITS], fp32, at)
    out_bias, at = place("out_bias", [P, C], fp32, at)
    query_bias, at = place("query_bias", [P, C], fp32, at)
    key_bias, at = place("key_bias", [P, C], fp32, at)
    shift, at_stages = place("shift", [P, B * TB], fp32, at)
    resid, at_t0 = place("resid", [P, B * TB, D], fp32, at_stages)
    t0_hi, at = place("t0_hi", [P, B, C, T], fp32r, at_t0)
    t0_lo, at_t1 = place("t0_lo", [P, B, C, T], fp32r, at)
    t1_hi, at = place("t1_hi", [P, B, C, T], fp32r, at_t1)
    t1_lo, at_rings = place("t1_lo", [P, B, C, T], fp32r, at)
    x2t_hi, at = place("x2t_hi", [P, B, C, T], fp16, at_rings)
    x2t_lo, at_end = place("x2t_lo", [P, B, C, T], fp16, at)
    TOP = 2 * C * P * 4
    a_raw, _ = place("a_raw", [P, DenseFetch.CHUNKS, T], fp32, END - TOP)
    ctx_raw, _ = place("ctx_raw", [P, ContextFetch.RING, BANK], fp32, END - TOP)
    gu, _ = place("gu", [P, 2, 2, C, P], fp16, END - TOP)
    dw_raw, _ = place("dw_raw", [P, 2, C, P], fp32, END - 2 * TOP)
    t0, t1, x2t = [t0_hi, t0_lo], [t1_hi, t1_lo], [x2t_hi, x2t_lo]

    with ExitStack() as semaphores:
        def stage_semaphores(scope):
            return lambda name: scope.enter_context(nc.semaphore(name))

        sem = stage_semaphores(semaphores)
        dense_fetch = DenseFetch(sem, dw_raw, a_raw, resid, {"dense": dense_w, "att_t": att_t, "x": x})
        context_fetch = ContextFetch(sem, ctx_raw, {"ctx": ctx})
        gate_up_fetch = GateUpFetch(sem, gu, {"gate_up": gate_up})
        attention(nc, sem, place, at_stages, at_t1, consts, qkv_bias, t0, dense_fetch,
                  {"x_t": x_t, "wqkv": wqkv, "consts": consts_in, "qkv_bias": qkv_bias_in, "att_t": att_t})
        dense(nc, sem, place, at_rings, dense_fetch, context_fetch, consts, out_bias, query_bias, key_bias, resid, t0, t1, shift,
              {"dense": dense_w, "att_t": att_t, "out_bias": out_bias_in,
               "query_bias": query_bias_in, "key_bias": key_bias_in})
        cross(nc, sem, place, at_t0, context_fetch, gate_up_fetch, x2t, consts, resid, t1, shift, {"ctx": ctx})
        ffn(nc, sem, place, at_t0, at_end, at_rings, gate_up_fetch, x2t, consts, resid,
            {"gate_up": gate_up, "down": down, "out": out})


def kernel(**inputs):
    import numpy as _np
    import concourse.bacc as _bacc
    from concourse import mybir as _mybir
    from concourse.bass_utils import run_bass_kernel_spmd as _run

    def array(name):
        return _np.asarray(inputs[name])

    def stationary(w):
        return w.reshape(w.shape[0] // P, P, C, P).transpose(0, 3, 2, 1)

    x, ctx = array("x"), array("ctx_4096")
    wk = array("L0_xattn_Wk").reshape(C, P, C, P).transpose(2, 1, 0, 3)
    gate_up = _np.stack([stationary(array("L0_ffn_W_gate")), stationary(array("L0_ffn_W_up"))], axis=2)
    ctx_t = ctx.transpose(0, 2, 1)
    streams = [a[b].reshape(C, P, HALVES, BANK).transpose(2, 0, 1, 3) for a in (ctx_t, ctx) for b in range(B)]

    eye = _np.eye(P, dtype=_np.float32)
    rows, cols = _np.arange(P)[:, None], _np.arange(P)[None, :]
    masked = _np.where(cols > rows, MASKED, 0.0)
    ramp = _np.broadcast_to(_np.arange(T) - (T - P), (P, T))
    slopes = 2.0 ** (-(_np.arange(H) + 1.0) * ALIBI_MAX / H) * float(HD) ** 0.5
    consts = _np.concatenate([eye, ramp, masked, _np.broadcast_to(_np.tile(slopes, B), (P, HEADS))], axis=1)

    laid_out = {
        "x_t": x.transpose(0, 2, 1).reshape(B, C, P, T),
        "x": x.reshape(B, TB, P, D),
        "ctx": _np.stack(streams).reshape(4 * B * C, P, BANK),
        "wqkv": array("L0_attn_w_qkv").reshape(3, NG, P, C, P).transpose(1, 0, 4, 3, 2).reshape(NG * 3, P, C * P),
        "dense": _np.concatenate([stationary(array("L0_attn_w_out")), stationary(array("L0_xattn_Wq")), wk]
                                 ).reshape(3 * C, P, C * P),
        "gate_up": gate_up.reshape(MB, P, 2 * C * P),
        "down": array("L0_ffn_W_down").T.reshape(MB // 2, 2, P, HALVES, BANK).transpose(3, 0, 2, 1, 4)
                .reshape(HALVES * MB // 2, P, 2 * BANK),
        "consts": consts.astype(_np.float32),
        "qkv_bias": _np.tile(array("L0_attn_b_qkv").reshape(3, NG, P).transpose(2, 0, 1), (1, 1, B)).reshape(P, 3 * UNITS),
        "out_bias": array("L0_attn_b_out").reshape(C, P).T,
        "query_bias": array("L0_xattn_bq").reshape(C, P).T,
        "key_bias": array("L0_xattn_bk").reshape(C, P).T,
    }
    nc = _bacc.Bacc("TRN2", target_bir_lowering=False, num_devices=1)
    arrays, args = {}, []
    for name, value in laid_out.items():
        value = _np.ascontiguousarray(value)
        arrays[f"in_{name}"] = value
        args.append(nc.dram_tensor(f"in_{name}", value.shape, _mybir.dt.from_np(value.dtype), kind="ExternalInput").ap())
    att_t = nc.dram_tensor("att_t_scratch", (UNITS, P, T), _mybir.dt.float32, kind="Internal").ap()
    out = nc.dram_tensor("out", (B, TB, P, D), _mybir.dt.float32, kind="ExternalOutput").ap()
    named = dict(zip(laid_out, args))
    decoder_layer(nc, named["x_t"], named["x"], named["ctx"], named["wqkv"], named["dense"], named["gate_up"],
                  named["down"], named["consts"], named["qkv_bias"], named["out_bias"], named["query_bias"],
                  named["key_bias"], att_t, out)
    result = _run(nc, [arrays], core_ids=[0])
    return result.results[0]["out"].reshape(B, T, D)
```

```python
import concourse.bass as bass
from concourse import mybir
from contextlib import ExitStack

B, T, D = 2, 512, 1024
H, HD = 32, 32
F = 3584
P = 128
C = D // P
TB = T // P
HG = P // HD
NG = H // HG
UNITS = B * NG
HEADS = UNITS * HG
EARLY = 6
MB = F // P
BANK = 512
HALVES = D // BANK
EPS = 1e-5
ALIBI_MAX = 8
PROB_UP = 2.0 ** 15
FP16_UP = 1024.0

PIECES = ((3,), (2, 0), (1,))
BLOCK_AT, PIECE_AT, HEAD_COLS = {}, [], 0
for _piece in PIECES:
    _first = HEAD_COLS
    for _i in _piece:
        BLOCK_AT[_i] = HEAD_COLS
        HEAD_COLS += P * (_i + 1)
    PIECE_AT.append((_first, HEAD_COLS))

HI, LO = 0, 1
PAIRS = ((HI, HI), (HI, LO), (LO, HI))

IDENT, RAMP, TRI, SLOPE = 0, P, P + T, P + T + P
CONSTS = SLOPE + HEADS
MASKED = -3e38


def wait(engine, semaphore, count):
    if not (isinstance(count, int) and count <= 0):
        engine.wait_ge(semaphore, count)


def attention(nc, sem, place, at, at_rest, consts, qkv_bias, x_half, dense_fetch, dram):
    fp32, fp32r = mybir.dt.float32, mybir.dt.float32r
    fp16, bf16 = mybir.dt.float16, mybir.dt.bfloat16
    ALU, ACT = mybir.AluOpType, mybir.ActivationFunctionType
    scale = float(HD) ** -0.5
    XR = 4
    Q, K, V = range(3)
    VP = 3

    def sb(name, shape, dtype):
        nonlocal at
        t, at = place(name, shape, dtype, at)
        return t

    x_raw = sb("x_raw", [P, XR, T], fp32)
    w_raw = sb("w_raw", [P, 3, C, P], fp32)
    w_half = [sb("w_hi", [P, 3, C, P], fp32r), None]
    at = at_rest
    w_half[LO] = sb("w_lo", [P, 3, C, P], fp32r)
    qk = sb("qk", [P, 4, T], fp32r)
    stack_at = at
    stack = sb("stack", [P, 2, HG, 2, T], fp32r)
    y_early, _ = place("y_early", [P, EARLY, T], fp32, stack_at)
    v_t = sb("v_t", [P, T], fp32)
    v = sb("v", [P, 2, TB, HG, VP, HD], bf16)
    v_rest = sb("v_rest", [P, TB, HG, HD], fp32)
    bias_tile = sb("bias_tile", [P, 2, T], fp32)
    probs = sb("probs", [P, 2, HEAD_COLS], fp32)
    pt_half = [sb("pt_hi", [P, 2, HEAD_COLS], fp16), sb("pt_lo", [P, 2, HEAD_COLS], fp16)]
    top = sb("top", [P, 2, TB], fp32)
    neg_top = sb("neg_top", [P, 2, TB], fp32)
    sums = sb("sums", [P, 2, HG, TB], fp32)
    inv_sums = sb("inv_sums", [P, 2, TB], fp32)
    o_sum = sb("o_sum", [P, 2, TB, HD], fp32)
    att = sb("att", [P, TB, HG, HD], fp32)
    att_t = sb("att_t", [P, T], fp32)
    zero = sb("zero", [P, 1], fp32)
    ident = consts[:, IDENT:IDENT + P]

    consts_in = sem("consts_in")
    x_in = [sem(f"x_in{k}") for k in range(XR)]
    x_hi_done = sem("x_hi_done")
    x_done = sem("x_done")
    w_in = [sem(f"w_in{k}") for k in range(3)]
    w_hi_done = sem("w_hi_done")
    w_done = sem("w_done")
    proj_done = sem("proj_done")
    qk_hi_done = sem("qk_hi_done")
    qk_done = sem("qk_done")
    stacked = [sem(f"stacked{j}") for j in range(HG)]
    v_t_done = sem("v_t_done")
    v_flipped = sem("v_flipped")
    v_first_done = sem("v_first_done")
    v_rest_done = sem("v_rest_done")
    v_second_done = sem("v_second_done")
    v_done = sem("v_done")
    ramp_done = sem("ramp_done")
    bias_done = sem("bias_done")
    scored = sem("scored")
    biased = sem("biased")
    top_done = sem("top_done")
    exp_done = sem("exp_done")
    flipped = sem("flipped")
    pt_hi_done = sem("pt_hi_done")
    pt_done = sem("pt_done")
    o_done = sem("o_done")
    o_sum_done = sem("o_sum_done")
    inv_done = sem("inv_done")
    att_done = sem("att_done")
    att_flipped = sem("att_flipped")
    att_t_done = sem("att_t_done")
    att_stored = dense_fetch.att_stored
    early_done = sem("early_done")
    biasing = sem("biasing")
    zero_done = sem("zero_done")

    LOOPS = ((4, NG, 0), (NG, UNITS - 2, 1))

    def steps(engine, step):
        for s in range(LOOPS[0][0]):
            step(s, s % 2, 0)
        for first, end, batch in LOOPS:
            with engine.Fori(0, (end - first) // 2) as i:
                step(i * 2 + first, 0, batch)
                step(i * 2 + (first + 1), 1, batch)
        for s in range(UNITS - 2, UNITS + 2):
            step(s, s % 2, 1 if s < UNITS else 0)

    SPLITS = {0: ((), (), (8, 9), (10, 11, 12, 13)), 1: ((), (), (), (14, 15))}
    LATE_SPLITS = {UNITS - 2: ((), (), (16, 17), (18, 19)), UNITS - 1: ((), (), (20, 21), (22, 23))}

    def has(s, unit_of_step):
        return not isinstance(s, int) or 0 <= s + unit_of_step < UNITS

    def works(s, unit_of_step):
        return not isinstance(s, int) or 0 <= s + unit_of_step < UNITS + EARLY // 3

    def settled(engine):
        engine.wait_ge(consts_in, 32)

    with ExitStack() as scope:
        def bank(name):
            return scope.enter_context(nc.psum_tensor(name, [P, BANK], fp32))

        proj = [bank("proj0"), bank("proj1")]
        score = [bank("score0"), bank("score1"), None]
        flip = [bank("flip0"), bank("flip1"), None]
        score[2], flip[2] = score[0], flip[0]
        o_ps = bank("o_ps")
        misc = bank("misc")
        o_parts = o_ps[:, 0:TB * VP * HD].rearrange("p (b x c) -> p b c x", b=TB, x=VP)
        misc_v = misc[:, :].rearrange("p (b h c) -> p b h c", b=TB, h=HG)

        block = scope.enter_context(nc.Block())

        @block.sync
        def _(sp):
            def load_x(n):
                wait(sp, x_done, n - XR + 1)
                source = dram["x_t"][n // C, n % C, :, :] if n < B * C else dram["att_t"][n - B * C, :, :]
                sp.dma_start(x_raw[:, n % XR, :], source).then_inc(x_in[n % XR], 16)

            def load_w(u, kind):
                wait(sp, w_done, (u - 1) * 3 + kind + 1)
                if isinstance(u, int) and u >= UNITS:
                    source = dram["dense"][(u - UNITS) * 3 + kind, :, :]
                else:
                    source = dram["wqkv"][bass.ds((u % NG) * 3 + kind, 1), :, :].rearrange("a p n -> p (a n)")
                sp.dma_start(w_raw[:, kind, :, :].rearrange("p c n -> p (c n)"), source).then_inc(w_in[kind], 16)

            load_w(0, Q)
            for n in range(XR):
                load_x(n)
            load_w(0, K)
            load_w(0, V)
            for n in range(XR, C):
                load_x(n)
            sp.dma_start(consts[:, :], dram["consts"]).then_inc(consts_in, 16)
            sp.dma_start(qkv_bias[:, :], dram["qkv_bias"]).then_inc(consts_in, 16)
            load_w(1, Q)
            for n in range(C, C + XR):
                load_x(n)
            load_w(1, K)

            def step(s, par, batch):
                if isinstance(s, int) and s in (UNITS - 2, UNITS - 1):
                    if s == UNITS - 2:
                        sp.wait_ge(att_stored, 16 * (s - 2))
                        dense_fetch.load_vectors(sp)
                    for n in range(C // 2):
                        load_x(B * C + (s - (UNITS - 2)) * C // 2 + n)
                if works(s, 1):
                    load_w(s + 1, V)
                if isinstance(s, int) and s == 0:
                    load_x(C + XR)
                    load_x(C + XR + 1)
                if has(s, 0):
                    wait(sp, qk_done, s * 2 + 2)
                    wait(sp, scored, (s - 1) * HG * 3)
                    for j in range(HG):
                        for r in range(4):
                            a, b = r // 2, 2 + r % 2
                            rows, to = slice(HD * j, HD * j + HD), slice(HD * r, HD * r + HD)
                            sp.dma_start(stack[to, par, j, :, :].bitcast(fp32),
                                         qk[rows, a:b + 1:b - a, :].bitcast(fp32)).then_inc(stacked[j], 16)
                if isinstance(s, int) and s == 0:
                    for n in range(C + XR + 2, B * C):
                        load_x(n)
                if works(s, 2):
                    load_w(s + 2, Q)
                    load_w(s + 2, K)
                if isinstance(s, int) and s == UNITS + 1:
                    sp.wait_ge(att_stored, 16 * (UNITS - 1))
                    sp.wait_ge(x_done, 3 * C)
                    sp.wait_ge(w_done, 3 * UNITS + EARLY)
                    dense_fetch.start(sp)
                if has(s, -2):
                    wait(sp, att_t_done, s - 1)
                    target = dram["att_t"][bass.ds(s - 2, 1), :, :].rearrange("a p n -> p (a n)")
                    sp.dma_start(target, att_t[:, :]).then_inc(att_stored, 16)

            steps(sp, step)

        @block.gpsimd
        def _(pool):
            def split_w(u, kind):
                pool.wait_ge(w_hi_done, u * 3 + kind + 1)
                nc.gpsimd.tensor_tensor(w_half[LO][:, kind, :, :], w_raw[:, kind, :, :],
                                        w_half[HI][:, kind, :, :].bitcast(fp32), ALU.subtract).then_inc(w_done, 1)

            def make_bias(h, slot):
                wait(pool, biased, (h - 1) * 3)
                settled(pool)
                nc.gpsimd.tensor_tensor(bias_tile[:, slot, :], consts[:, RAMP:RAMP + T],
                                        consts[:, bass.ds(h + SLOPE, 1)].broadcast_to([P, T]),
                                        ALU.mult).then_inc(ramp_done, 1)
                pool.wait_ge(ramp_done, h + 1)
                nc.gpsimd.tensor_tensor(bias_tile[:, slot, T - P:T], bias_tile[:, slot, T - P:T],
                                        consts[:, TRI:TRI + P], ALU.add).then_inc(bias_done, 1)

            def split_late(s, slot):
                if isinstance(s, int) and s in LATE_SPLITS:
                    for n in LATE_SPLITS[s][slot]:
                        pool.wait_ge(x_done, n)
                        pool.wait_ge(x_hi_done, n + 1)
                        nc.gpsimd.tensor_tensor(x_half[LO][:, 0, n % C, :], x_raw[:, n % XR, :],
                                                x_half[HI][:, 0, n % C, :].bitcast(fp32), ALU.subtract).then_inc(x_done, 1)

            split_w(0, K)
            split_w(0, V)

            def step(s, par, batch):
                if works(s, 0) and not (isinstance(s, int) and s == 0):
                    split_w(s, V)
                if has(s, -1):
                    pool.wait_ge(v_second_done, s)
                    nc.gpsimd.tensor_tensor(v[:, 1 - par, :, :, 2, :], v_rest[:, :, :, :],
                                            v[:, 1 - par, :, :, 1, :], ALU.subtract).then_inc(v_done, 1)
                if has(s, -1):
                    for j in range(1, HG):
                        make_bias((s - 1) * HG + j, j % 2)
                split_late(s, 2)
                if works(s, 1):
                    split_w(s + 1, Q)
                if has(s, 0):
                    make_bias(s * HG, 0)
                split_late(s, 3)
                if works(s, 1):
                    split_w(s + 1, K)

            steps(pool, step)

        @block.scalar
        def _(act):
            def split_w(u, kind):
                act.wait_ge(w_in[kind], u * 16 + 16)
                wait(act, proj_done, (u - 1) * 3 + kind + 1)
                nc.scalar.activation(w_half[HI][:, kind, :, :], w_raw[:, kind, :, :], ACT.Copy).then_inc(w_hi_done, 1)

            def split_x(n):
                act.wait_ge(x_in[n % XR], n // XR * 16 + 16)
                nc.scalar.activation(x_half[HI][:, n // C % B, n % C, :], x_raw[:, n % XR, :], ACT.Copy).then_inc(x_hi_done, 1)

            def bias_of(u, kind):
                return qkv_bias[:, bass.ds(u + kind * UNITS, 1)]

            act.wait_ge(zero_done, 1)
            nc.scalar.activation(zero[:, :], zero[:, :], ACT.Exp, bias=0.0, scale=0.0)
            split_w(0, Q)
            for n in range(XR):
                split_x(n)
            split_w(0, K)
            for n in range(XR, C):
                split_x(n)
            split_w(0, V)
            act.wait_ge(consts_in, 32)

            def step(s, par, batch):
                for j in range(HG):
                    if isinstance(s, int) and s in SPLITS:
                        for n in SPLITS[s][j]:
                            split_x(n)
                    if isinstance(s, int) and s in LATE_SPLITS:
                        for n in LATE_SPLITS[s][j]:
                            split_x(n)
                    if isinstance(s, int) and s == UNITS + 1 and j == 1:
                        nc.scalar.activation(zero[:, :], zero[:, :], ACT.Sqrt, bias=0.0, scale=0.0)
                    if j == 0 and has(s, -1):
                        act.wait_ge(proj_done, s * 3)
                        wait(act, v_flipped, s - 1)
                        settled(act)
                        nc.scalar.activation(v_t[:, :], proj[1 - par][:, :], ACT.Identity,
                                             bias=bias_of(s - 1, V)).then_inc(v_t_done, 1)
                    if j == 0 and isinstance(s, int) and s > UNITS:
                        early_out(s - 1, V)
                    if j == 0 and works(s, 0) and not (isinstance(s, int) and s == 0):
                        split_w(s, V)
                    if j == 1 and isinstance(s, int) and s >= UNITS:
                        early_out(s, Q)
                    if j == 3 and has(s, -2):
                        act.wait_ge(att_flipped, s - 1)
                        wait(act, att_stored, (s - 2) * 16)
                        nc.scalar.activation(att_t[:, :], misc[:, :], ACT.Copy, scale=1.0 / PROB_UP).then_inc(att_t_done, 1)
                    if has(s, -1 if j else -2):
                        h = (s - 1) * HG + j - 1
                        for k, (lo, hi) in enumerate(PIECE_AT):
                            act.wait_ge(flipped, h * 3 + k + 1)
                            if k == 0:
                                wait(act, o_done, h - 1)
                            nc.scalar.activation(pt_half[HI][:, (j - 1) % 2, lo:hi], flip[k][:, 0:hi - lo],
                                                 ACT.Copy, scale=PROB_UP).then_inc(pt_hi_done, 1)
                            if k == 0 and j == 1 and has(s, 0):
                                qk_hi(s, Q)
                            if k == 1 and j == 0 and has(s, -1):
                                v_first(s, par)
                            if k == 2 and j == 0 and has(s, -1):
                                v_second(s, par)
                    else:
                        if j == 1 and has(s, 0):
                            qk_hi(s, Q)
                        if j == 0 and has(s, -1):
                            v_first(s, par)
                            v_second(s, par)
                    if j == 2 and has(s, 0):
                        qk_hi(s, K)
                    if j == 2 and isinstance(s, int) and s >= UNITS:
                        early_out(s, K)
                    if j == 2 and works(s, 1):
                        split_w(s + 1, Q)
                    if j == 3 and works(s, 1):
                        split_w(s + 1, K)
                    if has(s, -1):
                        h = (s - 1) * HG + j
                        act.wait_ge(top_done, h + 1)
                        if j == 0:
                            wait(act, inv_done, (s - 2) * 2)
                        for i in (3, 2, 0, 1):
                            cols = probs[:, j % 2, BLOCK_AT[i]:BLOCK_AT[i] + P * (i + 1)]
                            last = nc.scalar.activation(cols, cols, ACT.Exp, bias=neg_top[:, j % 2, i:i + 1],
                                                        scale=scale, accum_out=sums[:, 1 - par, j, i:i + 1])
                        last.then_inc(exp_done, 1)

            def early_out(s, kind):
                n = (s - UNITS) * 3 + kind
                act.wait_ge(proj_done, UNITS * 3 + n + 1)
                if n == 0:
                    act.wait_ge(dense_fetch.vectors_in, 48)
                    act.wait_ge(scored, (UNITS - 1) * HG * 3)
                nc.scalar.activation(y_early[:, n, :], proj[(s + kind) % 2][:, :], ACT.Identity,
                                     bias=dense_fetch.out_bias[:, n:n + 1]).then_inc(early_done, 1)

            def v_first(s, par):
                act.wait_ge(v_flipped, s)
                wait(act, o_done, (s - 2) * HG)
                nc.scalar.activation(v[:, 1 - par, :, :, 0, :], misc_v, ACT.Copy).then_inc(v_first_done, 1)

            def v_second(s, par):
                act.wait_ge(v_rest_done, s)
                nc.scalar.activation(v[:, 1 - par, :, :, 1, :], v_rest[:, :, :, :], ACT.Copy).then_inc(v_second_done, 1)

            def qk_hi(s, kind):
                act.wait_ge(proj_done, s * 3 + kind + 1)
                if kind == Q:
                    for j in range(HG):
                        wait(act, stacked[j], s * 64)
                settled(act)
                nc.scalar.activation(qk[:, 2 * kind, :], proj[(par_of(s) + kind) % 2][:, :], ACT.Identity,
                                     bias=bias_of(s, kind)).then_inc(qk_hi_done, 1)

            current = [0]

            def par_of(s):
                return current[0]

            def step_with_parity(s, par, batch):
                current[0] = par
                step(s, par, batch)

            steps(act, step_with_parity)
            act.wait_ge(dense_fetch.w_in[0], 16)
            act.wait_ge(o_done, HEADS)
            nc.scalar.activation(dense_fetch.w_half[HI][:, 0, :, :], dense_fetch.w_raw[:, 0, :, :],
                                 ACT.Copy).then_inc(dense_fetch.w_hi_done, 1)
            early_out(UNITS + 1, V)

        @block.vector
        def _(dve):
            def split_x(n):
                dve.wait_ge(x_hi_done, n + 1)
                nc.vector.tensor_tensor(x_half[LO][:, n // C % B, n % C, :], x_raw[:, n % XR, :],
                                        x_half[HI][:, n // C % B, n % C, :].bitcast(fp32), ALU.subtract).then_inc(x_done, 1)

            nc.vector.memset(zero[:, :], 0.0).then_inc(zero_done, 1)
            dve.wait_ge(w_hi_done, 1)
            nc.vector.tensor_tensor(w_half[LO][:, Q, :, :], w_raw[:, Q, :, :],
                                    w_half[HI][:, Q, :, :].bitcast(fp32), ALU.subtract).then_inc(w_done, 1)
            for n in range(C):
                split_x(n)
            dve.wait_ge(consts_in, 32)

            def bias_scores(h, j, k):
                if k == 0:
                    dve.wait_ge(bias_done, h + 1)
                    wait(dve, flipped, (h - 1) * 3)
                dve.wait_ge(scored, h * 3 + k + 1)
                dve.sem_inc(biasing, 1)
                for i in PIECES[k]:
                    lo, width = BLOCK_AT[i], P * (i + 1)
                    first = lo - PIECE_AT[k][0]
                    last = nc.vector.tensor_tensor_reduce(
                        out=probs[:, j % 2, lo:lo + width], in0=score[k][:, first:first + width],
                        in1=bias_tile[:, j % 2, T - width:T], scale=1.0, scalar=MASKED,
                        op0=ALU.add, op1=ALU.max, accum_out=top[:, j % 2, i:i + 1])
                last.then_inc(biased, 1)

            def pt_lo(h, j, k):
                lo, hi = PIECE_AT[k]
                dve.wait_ge(pt_hi_done, h * 3 + k + 1)
                nc.vector.scalar_tensor_tensor(out=pt_half[LO][:, (j - 1) % 2, lo:hi], in0=flip[k][:, 0:hi - lo],
                                               scalar=PROB_UP, in1=pt_half[HI][:, (j - 1) % 2, lo:hi],
                                               op0=ALU.mult, op1=ALU.subtract).then_inc(pt_done, 1)

            def qk_lo(s, par, kind):
                dve.wait_ge(qk_hi_done, s * 2 + kind + 1)
                nc.vector.scalar_tensor_tensor(out=qk[:, 2 * kind + 1, :], in0=proj[(par + kind) % 2][:, :],
                                               scalar=qkv_bias[:, bass.ds(s + kind * UNITS, 1)],
                                               in1=qk[:, 2 * kind, :].bitcast(fp32),
                                               op0=ALU.add, op1=ALU.subtract).then_inc(qk_done, 1)

            def step(s, par, batch):
                for j in range(HG):
                    if isinstance(s, int) and s in SPLITS:
                        for n in SPLITS[s][j]:
                            split_x(n)
                    if has(s, -1 if j == 3 else -2):
                        head = (j - 3) % HG
                        dve.wait_ge(o_done, (s - 1) * HG + j - 2)
                        if head % 2 == 0:
                            wait(dve, att_done, ((s - 1) if j == 3 else (s - 2)) * 2 + head // 2)
                        nc.vector.tensor_reduce(o_sum[:, head % 2, :, :], o_parts, mybir.AxisListType.X,
                                                ALU.add).then_inc(o_sum_done, 1)
                    if j in (0, 2) and has(s, -2):
                        pair = (s - 2) * 2 + j // 2
                        nc.vector.reciprocal(inv_sums[:, :, :], sums[:, par, j:j + 2, :]).then_inc(inv_done, 1)
                        wait(dve, att_flipped, s - 2)
                        dve.wait_ge(inv_done, pair + 1)
                        dve.wait_ge(o_sum_done, pair * 2 + 2)
                        nc.vector.tensor_tensor(
                            att[:, :, j:j + 2, :], o_sum[:, :, :, :].rearrange("p h b c -> p b h c"),
                            inv_sums[:, :, :].rearrange("p h b -> p b h").unsqueeze(3).broadcast_to([P, TB, 2, HD]),
                            ALU.mult).then_inc(att_done, 1)
                    scores, flips = has(s, -1), has(s, -1 if j else -2)
                    h = (s - 1) * HG + j
                    if scores:
                        bias_scores(h, j, 0)
                        bias_scores(h, j, 1)
                    if flips:
                        pt_lo(h - 1, j, 0)
                    if j == 1 and has(s, 0):
                        qk_lo(s, par, Q)
                    if flips:
                        pt_lo(h - 1, j, 1)
                    if j == 0 and has(s, -1):
                        dve.wait_ge(v_first_done, s)
                        wait(dve, v_done, s - 1)
                        nc.vector.tensor_tensor(v_rest[:, :, :, :], misc_v, v[:, 1 - par, :, :, 0, :],
                                                ALU.subtract).then_inc(v_rest_done, 1)
                    if scores:
                        bias_scores(h, j, 2)
                        dve.wait_ge(biased, h * 3 + 3)
                        nc.vector.tensor_scalar(neg_top[:, j % 2, :], top[:, j % 2, :], -scale, None,
                                                ALU.mult).then_inc(top_done, 1)
                    if flips:
                        pt_lo(h - 1, j, 2)
                    if j == 2 and has(s, 0):
                        qk_lo(s, par, K)

            steps(dve, step)
            dve.wait_ge(dense_fetch.w_hi_done, 1)
            nc.vector.tensor_tensor(dense_fetch.w_half[LO][:, 0, :, :], dense_fetch.w_raw[:, 0, :, :],
                                    dense_fetch.w_half[HI][:, 0, :, :].bitcast(fp32),
                                    ALU.subtract).then_inc(dense_fetch.w_done, 1)

        @block.tensor
        def _(pe):
            def project(s, par, batch, products):
                for n in products:
                    kind, c, pair = n // (3 * C), n // 3 % C, n % 3
                    a, b = PAIRS[pair]
                    if n % (3 * C) == 0:
                        pe.wait_ge(w_done, s * 3 + kind + 1)
                        early = isinstance(s, int) and (s - UNITS) * 3 + kind
                        if early is not False and early >= 2:
                            pe.wait_ge(early_done, early - 1)
                        elif kind == V:
                            pe.wait_ge(qk_done, s * 2 + 1)
                        else:
                            wait(pe, (qk_done, v_t_done)[kind], (s * 2, s)[kind])
                        if kind == Q and not (isinstance(s, int) and s == 0):
                            pe.wait_ge(x_done, 3 * C if early is not False and early >= 0 else (batch + 1) * C)
                    if isinstance(s, int) and s == 0 and kind == Q and pair == 0:
                        pe.wait_ge(x_done, c + 1)
                    last = nc.tensor.matmul(proj[(par + kind) % 2][:, :], w_half[a][:, kind, c, :],
                                            x_half[b][:, batch, c, :], start=(n % (3 * C) == 0),
                                            stop=(n % (3 * C) == 3 * C - 1))
                    if n % (3 * C) == 3 * C - 1:
                        last.then_inc(proj_done, 1)

            def score_piece(h, j, unit_par, k):
                wait(pe, biased, h * 3 + (1 if k == 2 else 0))
                for i in PIECES[k]:
                    first, width = BLOCK_AT[i] - PIECE_AT[k][0], P * (i + 1)
                    last = nc.tensor.matmul(score[k][:, first:first + width], stack[:, unit_par, j, 0, P * i:P * i + P],
                                            stack[:, unit_par, j, 1, 0:width], start=True, stop=True)
                last.then_inc(scored, 1)

            def flip_piece(h, slot, k):
                if k == 0:
                    pe.wait_ge(exp_done, h + 1)
                wait(pe, pt_done, h * 3 + (1 if k == 2 else 0))
                lo, hi = PIECE_AT[k]
                for col in range(lo, hi, P):
                    last = nc.tensor.transpose(flip[k][:, col - lo:col - lo + P], probs[:, slot, col:col + P], ident)
                last.then_inc(flipped, 1)

            def step(s, par, batch):
                done = 0
                for j in range(HG):
                    scores, flips = has(s, -1), has(s, -1 if j else -2)
                    h = (s - 1) * HG + j

                    def project_next(count):
                        nonlocal done
                        if works(s, 0):
                            project(s, par, batch, range(done, done + count))
                            done += count

                    if isinstance(s, int) and s == 1 and j == 0:
                        project_next(12)
                    if scores:
                        pe.wait_ge(stacked[j], s * 64)
                        score_piece(h, j, 1 - par, 0)
                        score_piece(h, j, 1 - par, 1)
                    if not (isinstance(s, int) and s == 1 and j == 0):
                        project_next(6)
                    if j == 3 and has(s, -2):
                        pe.wait_ge(att_done, (s - 1) * 2)
                        pe.wait_ge(v_rest_done, min(s, UNITS) if isinstance(s, int) else s)
                        for b in range(TB):
                            last = nc.tensor.transpose(misc[:, P * b:P * b + P],
                                                       att[:, b, :, :].rearrange("p h c -> p (h c)"), ident)
                        last.then_inc(att_flipped, 1)
                    if flips:
                        flip_piece(h - 1, (j - 1) % 2, 0)
                        flip_piece(h - 1, (j - 1) % 2, 1)
                    if not (isinstance(s, int) and s == 1 and j == 0):
                        project_next(3)
                    if j == 0 and has(s, -1):
                        pe.wait_ge(v_t_done, s)
                        wait(pe, att_t_done, s - 2)
                        for b in range(TB):
                            last = nc.tensor.transpose(misc[:, P * b:P * b + P], v_t[:, P * b:P * b + P], ident)
                        last.then_inc(v_flipped, 1)
                    if scores:
                        score_piece(h, j, 1 - par, 2)
                    if not (isinstance(s, int) and s == 1 and j == 0):
                        project_next(3)
                    if flips:
                        flip_piece(h - 1, (j - 1) % 2, 2)
                    project_next(6)
                    if has(s, -1 if j >= 2 else -2):
                        head, unit_par = (j - 2) % HG, 1 - par if j >= 2 else par
                        pe.wait_ge(pt_done, (h - 2) * 3 + 3)
                        if head == 0:
                            pe.wait_ge(v_done, s)
                        wait(pe, o_sum_done, h - 2)
                        for i in range(TB):
                            for n in range(2 * (i + 1)):
                                key, half = n // 2, n % 2
                                col, first, parts = BLOCK_AT[i] + P * key, i * VP * HD, VP - half
                                last = nc.tensor.matmul(
                                    o_ps[:, first:first + parts * HD], pt_half[half][:, head % 2, col:col + P],
                                    v[:, unit_par, key, head, 0:parts, :].rearrange("p x c -> p (x c)"),
                                    start=(n == 0), stop=(n == 2 * i + 1))
                        last.then_inc(o_done, 1)

            steps(pe, step)

    return y_early


def layernorm_stats(nc, dve, x, first, stats, block, done):
    for half in range(HALVES):
        last = nc.vector.bn_stats(stats[:, block, half, :], x[:, first, BANK * half:BANK * half + BANK])
    last.then_inc(done, 1)


class DenseFetch:

    CHUNKS = 4

    def __init__(self, sem, w_raw, w_half, a_raw, resid, vectors, dram):
        self.w_half, self.w_hi_done, self.w_done = w_half, sem("dw_hi_done"), sem("dw_done")
        self.vectors, self.out_bias, self.vectors_in = vectors, vectors[0], sem("vectors_in")
        self.att_stored = sem("att_stored")
        self.resid, self.resid_in = resid, [sem(f"resid_in{b}") for b in range(B)]
        self.w_raw, self.a_raw, self.dram = w_raw, a_raw, dram
        self.w_in = [sem(f"dw_in{k}") for k in range(2)]
        self.a_in = [sem(f"a_in{k}") for k in range(self.CHUNKS)]

    def start(self, sp):
        for slot in range(2):
            sp.dma_start(self.w_raw[:, slot, :, :].rearrange("p c n -> p (c n)"),
                         self.dram["dense"][EARLY + slot, :, :]).then_inc(self.w_in[slot], 16)
        for n in range(self.CHUNKS):
            sp.dma_start(self.a_raw[:, n, :], self.dram["att_t"][C + n, :, :]).then_inc(self.a_in[n], 16)
        self.load_resid(sp, 0)

    def load_vectors(self, sp):
        for target, name in zip(self.vectors, ("out_bias", "query_bias", "key_bias")):
            sp.dma_start(target[:, :], self.dram[name]).then_inc(self.vectors_in, 16)

    def load_resid(self, sp, b):
        sp.dma_start(self.resid[:, b * TB:b * TB + TB, :],
                     self.dram["x"][b, :, :, :].rearrange("t p d -> p t d")).then_inc(self.resid_in[b], 16)


class ContextFetch:

    RING = 4

    def __init__(self, sem, ctx_raw, ctx_half, dram):
        self.raw, self.half, self.dram = ctx_raw, ctx_half, dram
        self.hi_done, self.split_done = sem("ctx_hi_done"), sem("ctx_done")
        self.done = [sem(f"ctx_in{k}") for k in range(self.RING)]

    def start(self, sp):
        for k in range(self.RING):
            sp.dma_start(self.raw[:, k, :], self.dram["ctx"][k, :, :]).then_inc(self.done[k], 16)


class GateUpFetch:

    def __init__(self, sem, gu, dram):
        self.gu, self.dram = gu, dram
        self.done = [sem(f"gu_in{k}") for k in range(2)]

    def start(self, sp, slot):
        sp.dma_start(self.gu[:, slot, :, :, :].rearrange("p g c n -> p (g c n)"),
                     self.dram["gate_up"][slot, :, :]).then_inc(self.done[slot], 16)


def dense(nc, sem, place, at, fetch, context_fetch, consts, y_early, out_bias, query_bias, key_bias, resid, t0_half, t1_half,
          shift, dram):
    fp32, fp32r = mybir.dt.float32, mybir.dt.float32r
    ALU, ACT = mybir.AluOpType, mybir.ActivationFunctionType
    OUT, QUERY, KEY = range(3)
    AR = DenseFetch.CHUNKS
    BLOCKS = 3 * B * C - EARLY

    def sb(name, shape, dtype):
        nonlocal at
        t, at = place(name, shape, dtype, at)
        return t

    w_half, w_hi_done, w_done = fetch.w_half, fetch.w_hi_done, fetch.w_done
    w_raw, a_raw = fetch.w_raw, fetch.a_raw
    y_t = sb("y_t", [P, 2, T], fp32)
    part = sb("part", [P, T], fp32)
    dot = sb("dot", [P, B, T], fp32)
    ones = sb("ones", [P, 2], fp32)
    stats = sb("stats", [P, TB, HALVES, 6], fp32)
    mean_var = sb("mean_var", [P, TB, 2], fp32)
    std = sb("std", [P, TB], fp32)
    eps = sb("eps", [P, 1], fp32)
    inv_std = sb("inv_std", [P, TB], fp32)
    ident = consts[:, IDENT:IDENT + P]

    vectors_in = fetch.vectors_in
    resid_in = fetch.resid_in
    a_in, w_in = fetch.a_in, fetch.w_in
    a_hi_done = sem("a_hi_done")
    a_done = sem("a_done")
    block_done = sem("block_done")
    y_done = sem("y_done")
    y_flipped = sem("y_flipped")
    y_added = sem("y_added")
    dot_zero = sem("dot_zero")
    ones_done = sem("ones_done")
    stats_done = sem("stats_done")
    aggr_done = sem("aggr_done")
    std_done = sem("std_done")
    inv_done = sem("inv_std_done")
    x1_done = sem("x1_done")
    x1_flipped = sem("x1_flipped")
    x1_hi_done = sem("x1_hi_done")
    x1_t_done = sem("x1_t_done")
    out_hi_done = sem("out_hi_done")
    out_done = sem("out_done")
    part_done = sem("part_done")
    dot_done = sem("dot_done")
    shift_ps_done = sem("shift_ps_done")
    shift_done = sem("shift_done")

    with ExitStack() as scope:
        def bank(name):
            return scope.enter_context(nc.psum_tensor(name, [P, BANK], fp32))

        acc = [bank("acc0"), bank("acc1")]
        y_ps = bank("y_ps")
        x1_ps = [bank("x1_ps0"), bank("x1_ps1")]
        shift_ps = [y_ps, bank("shift_ps")]
        block = scope.enter_context(nc.Block())

        def resid_cols(n):
            return bass.ds(n * P, P) if not isinstance(n, int) else slice(n * P, n * P + P)

        def at_block(n):
            return bass.ds(n, 1) if not isinstance(n, int) else slice(n, n + 1)

        @block.sync
        def _(sp):
            def load_w(w, slot, source):
                sp.wait_ge(w_done, w - EARLY - 1)
                sp.dma_start(w_raw[:, slot, :, :].rearrange("p c n -> p (c n)"),
                             dram["dense"][at_block(source), :, :].rearrange("a p n -> p (a n)")).then_inc(w_in[slot], 16)

            def load_a(n):
                sp.wait_ge(a_done, n - AR + 1)
                sp.dma_start(a_raw[:, n % AR, :], dram["att_t"][C + n, :, :]).then_inc(a_in[n % AR], 16)

            load_w(C, 0, 0)
            load_w(C + 1, 1, 1)
            sp.wait_ge(fetch.att_stored, 16 * UNITS)
            for n in range(AR, C):
                load_a(n)
            fetch.load_resid(sp, 1)
            for q in range(1, 3 * B):
                if q == 3 * B - 1:
                    sp.wait_ge(a_done, C)
                    context_fetch.start(sp)
                with sp.Fori(1 if q == 1 else 0, C // 2) as i:
                    for p in range(2):
                        load_w(i * 2 + (q * C + p), p, i * 2 + (q // B * C + p))

        @block.gpsimd
        def _(pool):
            def split_w(w, p):
                pool.wait_ge(w_hi_done, w + 1)
                nc.gpsimd.tensor_tensor(w_half[LO][:, p, :, :], w_raw[:, p, :, :],
                                        w_half[HI][:, p, :, :].bitcast(fp32), ALU.subtract).then_inc(w_done, 1)

            pool.wait_ge(w_done, 1)
            split_w(1, 1)
            with pool.Fori(1, BLOCKS // 2) as i:
                for p in range(2):
                    split_w(i * 2 + p, p)

        @block.scalar
        def _(act):
            def split_a(n):
                act.wait_ge(a_in[n % AR], n // AR * 16 + 16)
                nc.scalar.activation(t0_half[HI][:, 1, n, :], a_raw[:, n % AR, :], ACT.Copy).then_inc(a_hi_done, 1)

            def split_w(w, slot, turn):
                act.wait_ge(w_in[slot], turn * 16 + 16)
                wait(act, block_done, w - EARLY - 1)
                nc.scalar.activation(w_half[HI][:, slot, :, :], w_raw[:, slot, :, :], ACT.Copy).then_inc(w_hi_done, 1)

            def block_out(q, n, p):
                kind, b, w = q // B, q % B, n + q * C
                act.wait_ge(block_done, w - EARLY + 1)
                if kind == OUT:
                    if w >= EARLY + 2:
                        act.wait_ge(y_flipped, w - 1)
                    act.wait_ge(vectors_in, 48)
                    nc.scalar.activation(y_t[:, p, :], acc[p][:, :], ACT.Identity,
                                         bias=out_bias[:, at_block(n)]).then_inc(y_done, 1)
                else:
                    act.wait_ge(vectors_in, 48)
                    to = (t0_half if kind == QUERY else t1_half)[HI][:, b, at_block(n), :].rearrange("p a t -> p (a t)")
                    if kind == QUERY:
                        nc.scalar.activation(to, acc[p][:, :], ACT.Identity,
                                             bias=query_bias[:, at_block(n)]).then_inc(out_hi_done, 1)
                    else:
                        nc.scalar.activation(to, acc[p][:, :], ACT.Copy).then_inc(out_hi_done, 1)

            def x1_hi(b, c):
                act.wait_ge(x1_flipped, b * C + c + 1)
                nc.scalar.activation(t1_half[HI][:, b, c, :], x1_ps[c % 2][:, :], ACT.Copy).then_inc(x1_hi_done, 1)

            split_w(EARLY + 1, 1, 0)
            for n in range(AR):
                split_a(n)
            for q in range(3 * B):
                if q == 0:
                    for n in (C - 2, C - 1):
                        split_a(2 * (n - 4))
                        split_a(2 * (n - 4) + 1)
                        block_out(q, n, n % 2)
                        split_w(n + 2, n % 2, (n + 2 - EARLY) // 2)
                elif q > B:
                    if q == 3 * B - 1:
                        for k in range(ContextFetch.RING):
                            act.wait_ge(context_fetch.done[k], 16)
                            nc.scalar.activation(context_fetch.half[HI][:, k, :], context_fetch.raw[:, k, :],
                                                 ACT.Copy).then_inc(context_fetch.hi_done, 1)
                    count = C // 2 - (q == 3 * B - 1)
                    with act.Fori(0, count) as i:
                        for p in range(2):
                            n = i * 2 + p
                            block_out(q, n, p)
                            split_w(n + (q * C + 2), p, i + ((q * C + 2 - EARLY) // 2))
                    if count < C // 2:
                        block_out(q, C - 2, 0)
                        block_out(q, C - 1, 1)
                else:
                    normed = q - 1
                    for n in range(C):
                        block_out(q, n, n % 2)
                        split_w(q * C + n + 2, n % 2, (q * C + n + 2 - EARLY) // 2)
                        if n == 1:
                            act.wait_ge(ones_done, 1)
                            act.wait_ge(aggr_done, (normed + 1) * TB)
                            nc.scalar.activation(std[:, :], mean_var[:, :, 1], ACT.Sqrt, bias=eps[:, :]).then_inc(std_done, 1)
                        if n >= 4:
                            x1_hi(normed, (n - 4) * 2)
                            x1_hi(normed, (n - 4) * 2 + 1)
            act.wait_ge(ones_done, 1)
            nc.scalar.activation(std[:, 0:1], eps[:, :], ACT.Exp, bias=0.0)

        @block.vector
        def _(dve):
            def split_a(n):
                dve.wait_ge(a_hi_done, n + 1)
                nc.vector.tensor_tensor(t0_half[LO][:, 1, n, :], a_raw[:, n % AR, :],
                                        t0_half[HI][:, 1, n, :].bitcast(fp32), ALU.subtract).then_inc(a_done, 1)

            def add_y(b, n, w):
                dve.wait_ge(y_flipped, w + 1)
                dve.wait_ge(resid_in[b], 16)
                cols = resid[:, b * TB:b * TB + TB, resid_cols(n)]
                nc.vector.tensor_tensor(cols, y_ps[:, :].rearrange("p (t c) -> p t c", t=TB), cols, ALU.add).then_inc(y_added, 1)

            def block_lo(q, n, p):
                kind, b = q // B, q % B
                half = t0_half if kind == QUERY else t1_half
                hi = half[HI][:, b, at_block(n), :].rearrange("p a t -> p (a t)").bitcast(fp32)
                lo = half[LO][:, b, at_block(n), :].rearrange("p a t -> p (a t)")
                dve.wait_ge(out_hi_done, n + ((q - B) * C + 1))
                if kind == KEY:
                    nc.vector.tensor_tensor(lo, acc[p][:, :], hi, ALU.subtract).then_inc(out_done, 1)
                    return
                wait(dve, dot_done, n + (q - B) * C)
                nc.vector.tensor_scalar(part[:, :], acc[p][:, :], query_bias[:, at_block(n)], key_bias[:, at_block(n)],
                                        ALU.add, ALU.mult).then_inc(part_done, 1)
                nc.vector.scalar_tensor_tensor(out=lo, in0=acc[p][:, :], scalar=query_bias[:, at_block(n)], in1=hi,
                                               op0=ALU.add, op1=ALU.subtract).then_inc(out_done, 1)
                dve.wait_ge(part_done, n + ((q - B) * C + 1))
                nc.vector.tensor_tensor(dot[:, b, :], dot[:, b, :], part[:, :], ALU.add).then_inc(dot_done, 1)

            def x1_lo(b, c):
                dve.wait_ge(x1_hi_done, b * C + c + 1)
                nc.vector.tensor_tensor(t1_half[LO][:, b, c, :], x1_ps[c % 2][:, :],
                                        t1_half[HI][:, b, c, :].bitcast(fp32), ALU.subtract).then_inc(x1_t_done, 1)

            def norm_part(b, n):
                if n < 2:
                    for t in (2 * n, 2 * n + 1):
                        dve.wait_ge(y_added, (b + 1) * C)
                        if b:
                            dve.wait_ge(x1_done, b * TB)
                        layernorm_stats(nc, dve, resid, b * TB + t, stats, t, stats_done)
                        dve.wait_ge(stats_done, b * TB + t + 1)
                        nc.vector.bn_aggr(mean_var[:, t, :], stats[:, t, :, :].rearrange("p h s -> p (h s)")).then_inc(aggr_done, 1)
                elif n == 2:
                    dve.wait_ge(std_done, b + 1)
                    nc.vector.reciprocal(inv_std[:, :], std[:, :]).then_inc(inv_done, 1)
                    dve.wait_ge(inv_done, b + 1)
                if n in (2, 3):
                    for t in (2 * n - 4, 2 * n - 3):
                        rows = resid[:, b * TB + t, :]
                        nc.vector.tensor_scalar(rows, rows, mean_var[:, t, 0:1], inv_std[:, t:t + 1],
                                                ALU.subtract, ALU.mult).then_inc(x1_done, 1)

            for n in range(AR):
                split_a(n)
            for n in range(3):
                add_y(0, n, n)
            dve.wait_ge(fetch.att_stored, 16 * UNITS)
            nc.vector.memset(eps[:, :], EPS)
            nc.vector.memset(dot[:, :, :], 0.0).then_inc(dot_zero, 1)
            nc.vector.memset(ones[:, :], 1.0).then_inc(ones_done, 1)
            split_a(AR)
            split_a(AR + 1)
            for n in range(3, EARLY):
                add_y(0, n, n)
            split_a(AR + 2)
            split_a(AR + 3)
            for n in range(EARLY, C):
                add_y(0, n, n)
            for n in range(C):
                norm_part(0, n)
                if n >= 4:
                    x1_lo(0, (n - 4) * 2)
                    x1_lo(0, (n - 4) * 2 + 1)
                add_y(1, n, C + n)
            dve.wait_ge(vectors_in, 48)
            dve.wait_ge(dot_zero, 1)
            for n in range(C):
                norm_part(1, n)
                block_lo(B, n, n % 2)
                if n >= 4:
                    x1_lo(1, (n - 4) * 2)
                    x1_lo(1, (n - 4) * 2 + 1)
            for q in range(B + 1, 3 * B):
                if q == 3 * B - 1:
                    for k in range(ContextFetch.RING):
                        dve.wait_ge(context_fetch.hi_done, k + 1)
                        nc.vector.tensor_tensor(context_fetch.half[LO][:, k, :], context_fetch.raw[:, k, :],
                                                context_fetch.half[HI][:, k, :].bitcast(fp32),
                                                ALU.subtract).then_inc(context_fetch.split_done, 1)
                with dve.Fori(0, C // 2) as i:
                    for p in range(2):
                        block_lo(q, i * 2 + p, p)
            for b in range(B):
                dve.wait_ge(shift_ps_done, b + 1)
                nc.vector.tensor_copy(shift[:, b * TB:b * TB + TB], shift_ps[b][:, 0:TB]).then_inc(shift_done, 1)
            dve.wait_ge(shift_done, B)

        @block.tensor
        def _(pe):
            def products(q, n, p, first, end):
                kind, b, w = q // B, q % B, n + q * C
                moving = t1_half if kind == QUERY else t0_half
                if first == 0:
                    pe.wait_ge(w_done, w - EARLY + 1)
                    if kind == OUT or (isinstance(n, int) and n < 2 and q <= B):
                        wait(pe, y_done, w - EARLY - 1)
                    else:
                        wait(pe, out_done, w - (B * C + 1))
                for c in range(first, end):
                    if q == 1 and isinstance(n, int) and n == 0:
                        pe.wait_ge(a_done, c + 1)
                    if kind == QUERY and isinstance(n, int) and n == 0:
                        pe.wait_ge(x1_t_done, b * C + c + 1)
                    for k, (s, m) in enumerate(PAIRS):
                        last = nc.tensor.matmul(acc[p][:, :], w_half[s][:, p, c, :], moving[m][:, b, c, :],
                                                start=(c == 0 and k == 0), stop=(c == C - 1 and k == 2))
                if end == C:
                    last.then_inc(block_done, 1)

            def flip_y(w, p):
                early = isinstance(w, int) and w < EARLY
                if not early:
                    pe.wait_ge(y_done, w - EARLY + 1)
                wait(pe, y_added, w)
                for t in range(TB):
                    source = y_early[:, w, P * t:P * t + P] if early else y_t[:, p, P * t:P * t + P]
                    last = nc.tensor.transpose(y_ps[:, P * t:P * t + P], source, ident)
                last.then_inc(y_flipped, 1)

            def flip_x1(b, c):
                if c == 0:
                    pe.wait_ge(x1_done, (b + 1) * TB)
                wait(pe, x1_t_done, b * C + c - 1)
                for t in range(TB):
                    last = nc.tensor.transpose(x1_ps[c % 2][:, P * t:P * t + P],
                                               resid[:, b * TB + t, P * c:P * c + P], ident)
                last.then_inc(x1_flipped, 1)

            def sum_dot(b):
                pe.wait_ge(dot_done, (b + 1) * C)
                for t in range(TB):
                    last = nc.tensor.matmul(shift_ps[b][:, t:t + 1], dot[:, b, P * t:P * t + P],
                                            ones[:, 0:1], start=True, stop=True)
                last.then_inc(shift_ps_done, 1)

            def one_block(q, n, p, flips):
                products(q, n, p, 0, C // 2)
                if flips:
                    flip_y(n + (q * C - 1), 1 - p)
                products(q, n, p, C // 2, C)

            def block_between_flips(q, n, flips):
                for k, (first, end) in enumerate(((0, 3), (3, 6), (6, C))):
                    products(q, n, n % 2, first, end)
                    if k < len(flips):
                        flip_y(flips[k], flips[k] % 2)

            block_between_flips(0, C - 2, (0, 1, 2))
            block_between_flips(0, C - 1, (3, 4, 5))
            block_between_flips(1, 0, (6, 7))
            one_block(1, 1, 1, True)
            with pe.Fori(1, C // 4) as i:
                for p in range(2):
                    one_block(1, i * 2 + p, p, True)
            for n in range(C // 2, C):
                one_block(1, n, n % 2, True)
                flip_x1(0, 2 * (n - 4))
                flip_x1(0, 2 * (n - 4) + 1)
            for n in range(C):
                one_block(2, n, n % 2, n == 0)
                if n >= 4:
                    flip_x1(1, 2 * (n - 4))
                    flip_x1(1, 2 * (n - 4) + 1)
            one_block(3, 0, 0, False)
            one_block(3, 1, 1, False)
            with pe.Fori(1, C // 2) as i:
                for p in range(2):
                    one_block(3, i * 2 + p, p, False)
            for q in (4, 5):
                pe.wait_ge(out_done, (q - 3) * C)
                with pe.Fori(0, C // 2) as i:
                    for p in range(2):
                        one_block(q, i * 2 + p, p, False)
                if q == 4:
                    sum_dot(0)
            sum_dot(1)


def cross(nc, sem, place, at, at_rest, fetch, gate_up_fetch, x2t_half, consts, resid, t1_half, shift, dram):
    fp32, fp32r = mybir.dt.float32, mybir.dt.float32r
    ALU, ACT = mybir.AluOpType, mybir.ActivationFunctionType
    scale = float(D) ** -0.5
    RING = ContextFetch.RING
    PHASES = 4 * B
    CHUNKS = PHASES * C
    SCORES = 2 * B

    def sb(name, shape, dtype):
        nonlocal at
        t, at = place(name, shape, dtype, at)
        return t

    sx = sb("sx", [P, B, TB, D], fp32)
    at = at_rest
    ctx_raw = fetch.raw
    ctx_half = fetch.half
    top = sb("c_top", [P, B, TB], fp32)
    top_shift = sb("top_shift", [P, B, TB], fp32)
    exp_bias = sb("exp_bias", [P, B, TB], fp32)
    sums = sb("c_sums", [P, B, TB], fp32)
    inv_sums = sb("c_inv_sums", [P, B, TB], fp32)
    stats = sb("c_stats", [P, TB, HALVES, 6], fp32)
    mean_var = sb("c_mean_var", [P, TB, 2], fp32)
    std = sb("c_std", [P, TB], fp32)
    inv_std = sb("c_inv_std", [P, TB], fp32)
    eps = sb("c_eps", [P, 1], fp32)
    warm = sb("c_warm", [P, 1], fp32)
    ident = consts[:, IDENT:IDENT + P]

    ctx_in = fetch.done
    ctx_hi_done, ctx_done = fetch.hi_done, fetch.split_done
    ctx_used = sem("ctx_used")
    acc_done = sem("acc_done")
    s_out = sem("s_out")
    top_done = sem("c_top_done")
    top_shift_done = sem("top_shift_done")
    bias_done = sem("exp_bias_done")
    exp_done = sem("c_exp_done")
    inv_sums_done = sem("inv_sums_done")
    p_flipped = sem("p_flipped")
    p_hi_done = sem("p_hi_done")
    p_done = sem("p_done")
    av_out = sem("av_out")
    eps_done = sem("c_eps_done")
    stats_done = sem("c_stats_done")
    aggr_done = sem("c_aggr_done")
    std_done = sem("c_std_done")
    inv_done = sem("c_inv_done")
    x2_done = sem("x2_done")
    x2_flipped = sem("x2_flipped")
    x2_hi_done = sem("x2_hi_done")
    x2_t_done = sem("x2_t_done")

    with ExitStack() as scope:
        banks = [scope.enter_context(nc.psum_tensor(f"c_bank{k}", [P, BANK], fp32)) for k in range(8)]
        block = scope.enter_context(nc.Block())

        def bank_done(engine, phase, t):
            if t < TB - 1:
                engine.wait_ge(acc_done, phase * (TB - 1) + t + 1)
            else:
                engine.wait_ge(ctx_used, (phase + 1) * C)

        @block.sync
        def _(sp):
            def load(k, slot):
                wait(sp, ctx_done, k - RING + 1)
                sp.dma_start(ctx_raw[:, slot, :], dram["ctx"][bass.ds(k, 1), :, :].rearrange("a p n -> p (a n)")
                             ).then_inc(ctx_in[slot], 16)

            with sp.Fori(1, CHUNKS // RING) as i:
                for slot in range(RING):
                    load(i * RING + slot, slot)
            for slot in range(2):
                sp.wait_ge(ctx_done, CHUNKS - RING // 2 * (1 - slot))
                gate_up_fetch.start(sp, slot)

        @block.scalar
        def _(act):
            def split(k):
                act.wait_ge(ctx_in[k % RING], k // RING * 16 + 16)
                wait(act, ctx_used, k - RING + 1)
                nc.scalar.activation(ctx_half[HI][:, k % RING, :], ctx_raw[:, k % RING, :], ACT.Copy).then_inc(ctx_hi_done, 1)

            def after(phase, c):
                if c == C - 1 and phase < SCORES:
                    b, half = phase // 2, phase % 2
                    for t in range(TB):
                        bank_done(act, phase, t)
                        nc.scalar.activation(sx[:, b, t, BANK * half:BANK * half + BANK], banks[phase % 2 * TB + t][:, :],
                                             ACT.Copy).then_inc(s_out, 1)
                if phase in (2, 4) and c >= 4:
                    b, t = phase // 2 - 1, c - 4
                    act.wait_ge(bias_done, b + 1)
                    nc.scalar.activation(sx[:, b, t, :], sx[:, b, t, :], ACT.Exp, bias=exp_bias[:, b, t:t + 1],
                                         scale=scale, accum_out=sums[:, b, t:t + 1]).then_inc(exp_done, 1)
                if phase in (3, 5) and 1 <= c <= 4:
                    b = phase // 2 - 1
                    for n in (2 * c - 2, 2 * c - 1):
                        act.wait_ge(p_flipped, b * C + n + 1)
                        nc.scalar.activation(t1_half[HI][:, b, n, :], banks[n % 2][:, :], ACT.Copy).then_inc(p_hi_done, 1)
                if phase == 6 and c == 2:
                    act.wait_ge(aggr_done, TB)
                    nc.scalar.activation(std[:, :], mean_var[:, :, 1], ACT.Sqrt, bias=eps[:, :]).then_inc(std_done, 1)
                if phase == 7 and 1 <= c <= 4:
                    for n in (2 * c - 2, 2 * c - 1):
                        act.wait_ge(x2_flipped, n + 1)
                        nc.scalar.activation(x2t_half[HI][:, 0, n, :], banks[n % 2][:, :], ACT.Copy,
                                             scale=FP16_UP).then_inc(x2_hi_done, 1)

            act.wait_ge(eps_done, 1)
            for k in range(CHUNKS):
                if k + RING < CHUNKS:
                    split(k + RING)
                after(k // C, k % C)
            nc.scalar.activation(warm[:, :], eps[:, :], ACT.Silu)

        @block.vector
        def _(dve):
            def split(k):
                dve.wait_ge(ctx_hi_done, k + 1)
                nc.vector.tensor_tensor(ctx_half[LO][:, k % RING, :], ctx_raw[:, k % RING, :],
                                        ctx_half[HI][:, k % RING, :].bitcast(fp32), ALU.subtract).then_inc(ctx_done, 1)

            def after(phase, c):
                if phase in (2, 4) and c < TB:
                    b = phase // 2 - 1
                    dve.wait_ge(s_out, (phase - 1) * TB + c + 1)
                    nc.vector.tensor_reduce(top[:, b, c:c + 1], sx[:, b, c, :], mybir.AxisListType.X,
                                            ALU.max).then_inc(top_done, 1)
                if phase in (2, 4) and c == TB - 1:
                    b = phase // 2 - 1
                    rows = shift[:, b * TB:b * TB + TB]
                    dve.wait_ge(top_done, (b + 1) * TB)
                    nc.vector.tensor_tensor(top_shift[:, b, :], top[:, b, :], rows, ALU.add).then_inc(top_shift_done, 1)
                    dve.wait_ge(top_shift_done, 2 * b + 1)
                    nc.vector.tensor_tensor(top_shift[:, b, :], rows, top_shift[:, b, :], ALU.subtract).then_inc(top_shift_done, 1)
                    dve.wait_ge(top_shift_done, 2 * b + 2)
                    nc.vector.tensor_scalar(exp_bias[:, b, :], top_shift[:, b, :], scale, None, ALU.mult).then_inc(bias_done, 1)
                if phase in (3, 5) and c == 0:
                    b = phase // 2 - 1
                    dve.wait_ge(exp_done, (b + 1) * TB)
                    nc.vector.reciprocal(inv_sums[:, b, :], sums[:, b, :]).then_inc(inv_sums_done, 1)
                if phase in (3, 5) and 1 <= c <= 4:
                    b = phase // 2 - 1
                    for n in (2 * c - 2, 2 * c - 1):
                        dve.wait_ge(p_hi_done, b * C + n + 1)
                        nc.vector.tensor_tensor(t1_half[LO][:, b, n, :], banks[n % 2][:, :],
                                                t1_half[HI][:, b, n, :].bitcast(fp32), ALU.subtract).then_inc(p_done, 1)
                if c == C - 1 and phase >= SCORES:
                    b, half = (phase - SCORES) // 2, phase % 2
                    dve.wait_ge(inv_sums_done, b + 1)
                    for t in range(TB):
                        bank_done(dve, phase, t)
                        cols = resid[:, b * TB + t, BANK * half:BANK * half + BANK]
                        nc.vector.scalar_tensor_tensor(out=cols, in0=banks[phase % 2 * TB + t][:, :],
                                                       scalar=inv_sums[:, b, t:t + 1], in1=cols,
                                                       op0=ALU.mult, op1=ALU.add).then_inc(av_out, 1)
                if phase == 6 and c < 2:
                    for t in (2 * c, 2 * c + 1):
                        dve.wait_ge(av_out, 2 * TB)
                        layernorm_stats(nc, dve, resid, t, stats, t, stats_done)
                        dve.wait_ge(stats_done, t + 1)
                        nc.vector.bn_aggr(mean_var[:, t, :], stats[:, t, :, :].rearrange("p h s -> p (h s)")).then_inc(aggr_done, 1)
                if phase == 6 and c == 3:
                    dve.wait_ge(std_done, 1)
                    nc.vector.reciprocal(inv_std[:, :], std[:, :]).then_inc(inv_done, 1)
                    dve.wait_ge(inv_done, 1)
                if phase == 6 and c in (3, 4):
                    for t in (2 * c - 6, 2 * c - 5):
                        nc.vector.tensor_scalar(resid[:, t, :], resid[:, t, :], mean_var[:, t, 0:1], inv_std[:, t:t + 1],
                                                ALU.subtract, ALU.mult).then_inc(x2_done, 1)
                if phase == 7 and 1 <= c <= 4:
                    for n in (2 * c - 2, 2 * c - 1):
                        dve.wait_ge(x2_hi_done, n + 1)
                        nc.vector.scalar_tensor_tensor(out=x2t_half[LO][:, 0, n, :], in0=banks[n % 2][:, :], scalar=FP16_UP,
                                                       in1=x2t_half[HI][:, 0, n, :], op0=ALU.mult,
                                                       op1=ALU.subtract).then_inc(x2_t_done, 1)

            nc.vector.memset(eps[:, :], EPS).then_inc(eps_done, 1)
            for k in range(CHUNKS):
                if k + RING < CHUNKS:
                    split(k + RING)
                after(k // C, k % C)

        @block.tensor
        def _(pe):
            for phase in range(PHASES):
                attends = phase >= SCORES
                b = (phase - SCORES) // 2 if attends else phase // 2
                if phase in (2, 3):
                    pe.wait_ge(s_out, (phase - 1) * TB)
                elif phase == 4:
                    pe.wait_ge(p_done, C)
                elif phase == 5:
                    pe.wait_ge(s_out, SCORES * TB)
                elif phase == 6:
                    pe.wait_ge(p_done, 2 * C)
                elif phase == 7:
                    pe.wait_ge(av_out, 2 * TB)
                for c in range(C):
                    k = phase * C + c
                    pe.wait_ge(ctx_done, k + 1)
                    for t in range(TB):
                        for n, (s, m) in enumerate(PAIRS):
                            last = nc.tensor.matmul(banks[phase % 2 * TB + t][:, :], t1_half[s][:, b, c, P * t:P * t + P],
                                                    ctx_half[m][:, k % RING, :], start=(c == 0 and n == 0),
                                                    stop=(c == C - 1 and n == 2))
                        if c == C - 1 and t < TB - 1:
                            last.then_inc(acc_done, 1)
                    last.then_inc(ctx_used, 1)
                    if phase in (3, 5) and 1 <= c <= 4:
                        pb = phase // 2 - 1
                        if c == 1:
                            if pb == 0:
                                pe.wait_ge(s_out, 3 * TB)
                            else:
                                pe.wait_ge(av_out, TB)
                            pe.wait_ge(exp_done, (pb + 1) * TB)
                        for n in (2 * c - 2, 2 * c - 1):
                            wait(pe, p_done, pb * C + n - 1)
                            for t in range(TB):
                                last = nc.tensor.transpose(banks[n % 2][:, P * t:P * t + P], sx[:, pb, t, P * n:P * n + P], ident)
                            last.then_inc(p_flipped, 1)
                    if phase == 7 and 1 <= c <= 4:
                        if c == 1:
                            pe.wait_ge(av_out, 3 * TB)
                            pe.wait_ge(x2_done, TB)
                        for n in (2 * c - 2, 2 * c - 1):
                            wait(pe, x2_t_done, n - 1)
                            for t in range(TB):
                                last = nc.tensor.transpose(banks[n % 2][:, P * t:P * t + P], resid[:, t, P * n:P * n + P], ident)
                            last.then_inc(x2_flipped, 1)


def ffn(nc, sem, place, at, top, x2t_at, fetch, x2t_half, consts, resid, dram):
    fp32, fp32r, fp16 = mybir.dt.float32, mybir.dt.float32r, mybir.dt.float16
    ALU, ACT = mybir.AluOpType, mybir.ActivationFunctionType
    PEELED = 8
    DOWN = HALVES * MB
    WD = 4
    LAST = 8
    DOWN_UP = 1.0 / FP16_UP

    def sb(name, shape, dtype):
        nonlocal at
        t, at = place(name, shape, dtype, at)
        return t

    h_half = [sb("h_hi", [P, MB, T], fp32r), sb("h_lo", [P, MB, T], fp32r)]
    wd_last, _ = place("wd_last", [P, LAST, BANK], fp32r, x2t_at)
    gu = fetch.gu
    wd = sb("wd", [P, WD, BANK], fp32r)
    wd_raw = sb("wd_raw", [P, 2, 2, BANK], fp16)
    gated = sb("gated", [P, 2, T], fp32)
    at = top
    stats = sb("f_stats", [P, TB, HALVES, 6], fp32)
    mean_var = sb("f_mean_var", [P, TB, 2], fp32)
    std = sb("f_std", [P, TB], fp32)
    inv_std = sb("f_inv_std", [P, TB], fp32)
    eps = sb("f_eps", [P, 1], fp32)
    ident = consts[:, IDENT:IDENT + P]

    gu_in = fetch.done
    wd_in = [sem(f"wd_in{k}") for k in range(2)]
    gate_done = sem("gate_done")
    up_done = sem("up_done")
    silu_done = sem("silu_done")
    gated_done = sem("gated_done")
    h_hi_done = sem("h_hi_done")
    h_done = sem("h_done")
    wd_done = sem("wd_done")
    wd_used = sem("wd_used")
    down_done = sem("down_done")
    down_out = sem("down_out")
    last_done = sem("last_done")
    eps_done = sem("f_eps_done")
    first_stats_done = sem("first_stats_done")
    stats_done = sem("f_stats_done")
    aggr_done = sem("f_aggr_done")
    std_done = sem("f_std_done")
    inv_done = sem("f_inv_done")
    norm_done = sem("norm_done")
    x2_flipped = sem("f_x2_flipped")
    x2_hi_done = sem("f_x2_hi_done")
    x2_t_done = sem("f_x2_t_done")
    stored = sem("stored")

    def at_block(n):
        return slice(n, n + 1) if isinstance(n, int) else bass.ds(n, 1)

    with ExitStack() as scope:
        banks = [scope.enter_context(nc.psum_tensor(f"f_bank{k}", [P, BANK], fp32)) for k in range(8)]
        block = scope.enter_context(nc.Block())

        def gate_bank(b, p):
            return banks[4 * b + 2 * p]

        def up_bank(b, p):
            return banks[4 * b + 2 * p + 1]

        def down_bank(b, half, t):
            return banks[4 * ((b + half + 1) % 2) + t]

        @block.sync
        def _(sp):
            def load_gu(b, m, p, turn):
                wait(sp, up_done, b * MB + m - 1)
                sp.dma_start(gu[:, p, :, :, :].rearrange("p g c n -> p (g c n)"),
                             dram["gate_up"][at_block(m), :, :].rearrange("a p n -> p (a n)")).then_inc(gu_in[p], 16)

            def load_wd(b, pair, p):
                wait(sp, wd_done, b * DOWN + pair * 2 - 2)
                sp.dma_start(wd_raw[:, p, :, :].rearrange("p k n -> p (k n)"),
                             dram["down"][at_block(pair), :, :].rearrange("a p n -> p (a n)")).then_inc(wd_in[p], 16)

            def store(b):
                for t in range(TB):
                    sp.wait_ge(norm_done, (b + 1) * TB + t + 1)
                    sp.dma_start(dram["out"][b, t, :, :], resid[:, b * TB + t, :]).then_inc(stored, 16)

            for b in range(B):
                for m in range(0 if b else 2, PEELED):
                    load_gu(b, m, m % 2, 0)
                load_wd(b, 0, 0)
                load_wd(b, 1, 1)
                if b == 1:
                    store(0)
                with sp.Fori(PEELED // 2, MB // 2) as i:
                    for p in range(2):
                        load_gu(b, i * 2 + p, p, i)
                with sp.Fori(1, DOWN // 4) as i:
                    for p in range(2):
                        load_wd(b, i * 2 + p, p)
            store(1)
            sp.wait_ge(stored, 16 * B * TB)

        @block.scalar
        def _(act):
            def step(b, m, p):
                act.wait_ge(gate_done, b * MB + m + 1)
                wait(act, h_done, b * MB + m - 1)
                nc.scalar.activation(gated[:, p, :], gate_bank(b, p)[:, :], ACT.Silu, scale=DOWN_UP).then_inc(silu_done, 1)
                act.wait_ge(gated_done, b * MB + m + 1)
                act.wait_ge(eps_done, 1)
                nc.scalar.activation(h_half[HI][:, at_block(m), :].rearrange("p a t -> p (a t)"), gated[:, p, :],
                                     ACT.Copy).then_inc(h_hi_done, 1)

            def convert(b, i, n):
                if n % 2 == 0:
                    act.wait_ge(wd_in[n // 2], i * 16 + (b * DOWN // 4 * 16 + 16))
                wait(act, wd_used, i * WD + (b * DOWN + n - WD + 1))
                nc.scalar.activation(wd[:, n, :], wd_raw[:, n // 2, n % 2, :], ACT.Copy).then_inc(wd_done, 1)

            def square_root(turn):
                act.wait_ge(aggr_done, (turn + 1) * TB)
                nc.scalar.activation(std[:, :], mean_var[:, :, 1], ACT.Sqrt, bias=eps[:, :]).then_inc(std_done, 1)

            act.wait_ge(eps_done, 1)
            for b in range(B):
                for m in range(PEELED):
                    step(b, m, m % 2)
                    if m == 1:
                        square_root(b)
                    if b == 0 and m >= PEELED - C // 2:
                        for c in (2 * m - 2 * PEELED + C, 2 * m - 2 * PEELED + C + 1):
                            act.wait_ge(x2_flipped, c + 1)
                            nc.scalar.activation(x2t_half[HI][:, 1, c, :], banks[4 + c % 2][:, :], ACT.Copy,
                                                 scale=FP16_UP).then_inc(x2_hi_done, 1)
                for n in range(WD):
                    convert(b, 0, n)
                with act.Fori(PEELED // 2, MB // 2) as i:
                    for p in range(2):
                        step(b, i * 2 + p, p)
                with act.Fori(1, (DOWN - (LAST if b == B - 1 else 0)) // WD) as i:
                    for n in range(WD):
                        convert(b, i, n)
            for n in range(LAST):
                pair = (B * DOWN - LAST + n) // 2
                act.wait_ge(wd_in[pair % 2], pair // 2 * 16 + 16)
                nc.scalar.activation(wd_last[:, n, :], wd_raw[:, pair % 2, n % 2, :], ACT.Copy).then_inc(wd_done, 1)
            for t in range(TB):
                act.wait_ge(aggr_done, 2 * TB + t + 1)
                nc.scalar.activation(std[:, t:t + 1], mean_var[:, t, 1:2], ACT.Sqrt, bias=eps[:, :]).then_inc(std_done, 1)

        @block.vector
        def _(dve):
            def step(b, m, p):
                dve.wait_ge(silu_done, b * MB + m + 1)
                dve.wait_ge(up_done, b * MB + m + 1)
                nc.vector.scalar_tensor_tensor(out=gated[:, p, :], in0=up_bank(b, p)[:, :], scalar=DOWN_UP,
                                               in1=gated[:, p, :], op0=ALU.mult, op1=ALU.mult).then_inc(gated_done, 1)
                dve.wait_ge(h_hi_done, b * MB + m + 1)
                nc.vector.tensor_tensor(h_half[LO][:, at_block(m), :].rearrange("p a t -> p (a t)"), gated[:, p, :],
                                        h_half[HI][:, at_block(m), :].rearrange("p a t -> p (a t)").bitcast(fp32),
                                        ALU.subtract).then_inc(h_done, 1)

            def norm_stats(turn, t):
                first = (1, 0, 1)[turn] * TB + t
                wait(dve, down_out, turn * 2 * TB)
                wait(dve, norm_done, turn * TB)
                layernorm_stats(nc, dve, resid, first, stats, t, stats_done)
                dve.wait_ge(stats_done, turn * TB + t + 1)
                nc.vector.bn_aggr(mean_var[:, t, :], stats[:, t, :, :].rearrange("p h s -> p (h s)")).then_inc(aggr_done, 1)

            def inverse(turn):
                dve.wait_ge(std_done, turn + 1)
                nc.vector.reciprocal(inv_std[:, :], std[:, :]).then_inc(inv_done, 1)
                dve.wait_ge(inv_done, turn + 1)

            def normalise(turn, t):
                rows = resid[:, (1, 0, 1)[turn] * TB + t, :]
                nc.vector.tensor_scalar(rows, rows, mean_var[:, t, 0:1], inv_std[:, t:t + 1],
                                        ALU.subtract, ALU.mult).then_inc(norm_done, 1)

            def down(b, half):
                for t in range(TB):
                    turn = b * HALVES + half
                    if t < TB - 1:
                        dve.wait_ge(down_done, turn * (TB - 1) + t + 1)
                    else:
                        dve.wait_ge(wd_used, (turn + 1) * MB)
                    wait(dve, norm_done, (b + 1) * TB if b == 0 else 0)
                    cols = resid[:, b * TB + t, BANK * half:BANK * half + BANK]
                    nc.vector.tensor_tensor(cols, down_bank(b, half, t)[:, :], cols, ALU.add).then_inc(down_out, 1)

            nc.vector.memset(eps[:, :], EPS).then_inc(eps_done, 1)
            for b in range(B):
                for m in range(PEELED):
                    if m < 2:
                        norm_stats(b, 2 * m)
                        norm_stats(b, 2 * m + 1)
                    step(b, m, m % 2)
                    if m == 2:
                        inverse(b)
                    if m in (2, 3):
                        normalise(b, 2 * m - 4)
                        normalise(b, 2 * m - 3)
                    if b == 0 and m >= PEELED - C // 2:
                        for c in (2 * m - 2 * PEELED + C, 2 * m - 2 * PEELED + C + 1):
                            dve.wait_ge(x2_hi_done, c + 1)
                            nc.vector.scalar_tensor_tensor(out=x2t_half[LO][:, 1, c, :], in0=banks[4 + c % 2][:, :],
                                                           scalar=FP16_UP, in1=x2t_half[HI][:, 1, c, :],
                                                           op0=ALU.mult, op1=ALU.subtract).then_inc(x2_t_done, 1)
                with dve.Fori(PEELED // 2, MB // 2) as i:
                    for p in range(2):
                        step(b, i * 2 + p, p)
                down(b, 0)
                if b == 0:
                    down(b, 1)
            dve.wait_ge(down_out, (2 * B - 1) * TB)
            dve.wait_ge(norm_done, 2 * TB)
            for t in range(TB):
                nc.vector.bn_stats(stats[:, t, 0, :], resid[:, TB + t, 0:BANK]).then_inc(first_stats_done, 1)
            for t in range(TB):
                dve.wait_ge(last_done, t + 1)
                cols = resid[:, TB + t, BANK:D]
                nc.vector.tensor_tensor(cols, down_bank(1, 1, t)[:, :], cols, ALU.add).then_inc(down_out, 1)
                dve.wait_ge(down_out, (2 * B - 1) * TB + t + 1)
                nc.vector.bn_stats(stats[:, t, 1, :], cols).then_inc(stats_done, 1)
                dve.wait_ge(first_stats_done, t + 1)
                dve.wait_ge(stats_done, 2 * TB + t + 1)
                nc.vector.bn_aggr(mean_var[:, t, :], stats[:, t, :, :].rearrange("p h s -> p (h s)")).then_inc(aggr_done, 1)
                dve.wait_ge(std_done, 3 + t)
                nc.vector.reciprocal(inv_std[:, t:t + 1], std[:, t:t + 1]).then_inc(inv_done, 1)
                dve.wait_ge(inv_done, 3 + t)
                normalise(2, t)

        @block.tensor
        def _(pe):
            def step(b, m, p, turn):
                pe.wait_ge(gu_in[p], turn * 16 + (b * MB // 2 * 16 + 16))
                for g, (bank, done) in enumerate(((gate_bank(b, p), gate_done), (up_bank(b, p), up_done))):
                    if not (isinstance(m, int) and m < 2):
                        wait(pe, (silu_done, gated_done)[g], b * MB + m - 1)
                    for c in range(C):
                        for half in (HI, LO):
                            last = nc.tensor.matmul(bank[:, :], gu[:, p, g, c, :], x2t_half[half][:, b, c, :],
                                                    start=(c == 0 and half == HI), stop=(c == C - 1 and half == LO))
                    last.then_inc(done, 1)

            def flip_x2(c):
                pe.wait_ge(norm_done, TB)
                wait(pe, x2_t_done, c - 1)
                for t in range(TB):
                    last = nc.tensor.transpose(banks[4 + c % 2][:, P * t:P * t + P],
                                               resid[:, TB + t, P * c:P * c + P], ident)
                last.then_inc(x2_flipped, 1)

            for b in range(B):
                if b == 1:
                    pe.wait_ge(x2_t_done, C)
                    pe.wait_ge(down_out, TB)
                for m in range(PEELED):
                    step(b, m, m % 2, m // 2)
                    if b == 0 and m >= PEELED - C // 2:
                        flip_x2(2 * m - 2 * PEELED + C)
                        flip_x2(2 * m - 2 * PEELED + C + 1)
                with pe.Fori(PEELED // 2, MB // 2) as i:
                    for p in range(2):
                        step(b, i * 2 + p, p, i)
                for half in range(HALVES):
                    if half == 0:
                        if b == 0:
                            pe.wait_ge(x2_t_done, C)
                        else:
                            pe.wait_ge(down_out, 2 * TB)
                    else:
                        pe.wait_ge(gated_done, (b + 1) * MB)
                    straight = LAST if b == B - 1 and half == 1 else 0
                    for m in range(MB - straight):
                        k = half * MB + m
                        pe.wait_ge(wd_done, b * DOWN + k + 1)
                        if half == 0:
                            pe.wait_ge(h_done, b * MB + m + 1)
                        for t in range(TB):
                            for a in (HI, LO):
                                last = nc.tensor.matmul(down_bank(b, half, t)[:, :], h_half[a][:, m, P * t:P * t + P],
                                                        wd[:, k % WD, :], start=(m == 0 and a == HI),
                                                        stop=(m == MB - 1 and a == LO))
                            if m == MB - 1 and t < TB - 1:
                                last.then_inc(down_done, 1)
                        last.then_inc(wd_used, 1)
            for t in range(TB):
                for n in range(LAST):
                    if t == 0:
                        pe.wait_ge(wd_done, B * DOWN - LAST + n + 1)
                    for a in (HI, LO):
                        last = nc.tensor.matmul(down_bank(1, 1, t)[:, :], h_half[a][:, MB - LAST + n, P * t:P * t + P],
                                                wd_last[:, n, :], start=False, stop=(n == LAST - 1 and a == LO))
                last.then_inc(last_done, 1)


def decoder_layer(nc, x_t, x, ctx, wqkv, dense_w, gate_up, down, consts_in, qkv_bias_in, out_bias_in,
                  query_bias_in, key_bias_in, att_t, out):
    fp32, fp32r, fp16 = mybir.dt.float32, mybir.dt.float32r, mybir.dt.float16
    FIRST, END = 16512, 229344
    SIZES = {fp32: 4, fp32r: 4, fp16: 2, mybir.dt.bfloat16: 2}

    def place(name, shape, dtype, at):
        size = SIZES[dtype]
        for extent in shape[1:]:
            size *= extent
        after = (at + size + 31) // 32 * 32
        assert after <= END, (name, after)
        return nc.alloc_sbuf_tensor_at(name, shape, dtype, offset=at), after

    consts, at = place("consts", [P, CONSTS], fp32, FIRST)
    qkv_bias, at = place("qkv_bias", [P, 3 * UNITS], fp32, at)
    out_bias, at = place("out_bias", [P, C], fp32, at)
    query_bias, at = place("query_bias", [P, C], fp32, at)
    key_bias, at = place("key_bias", [P, C], fp32, at)
    shift, at_stages = place("shift", [P, B * TB], fp32, at)
    resid, at_t0 = place("resid", [P, B * TB, D], fp32, at_stages)
    t0_hi, t0_lo_at = place("t0_hi", [P, B, C, T], fp32r, at_t0)
    t0_lo, at_t1 = place("t0_lo", [P, B, C, T], fp32r, t0_lo_at)
    t1_hi, at = place("t1_hi", [P, B, C, T], fp32r, at_t1)
    t1_lo, at_rings = place("t1_lo", [P, B, C, T], fp32r, at)
    x2t_hi, at = place("x2t_hi", [P, B, C, T], fp16, at_rings)
    x2t_lo, at_end = place("x2t_lo", [P, B, C, T], fp16, at)
    dw_hi, at = place("dw_hi", [P, 2, C, P], fp32r, at_rings)
    dw_lo, at_dense = place("dw_lo", [P, 2, C, P], fp32r, at)
    ctx_hi, at = place("ctx_hi", [P, ContextFetch.RING, BANK], fp32r, t0_lo_at)
    ctx_lo, at = place("ctx_lo", [P, ContextFetch.RING, BANK], fp32r, at)
    at_cross = at
    TOP = 2 * C * P * 4
    a_raw, _ = place("a_raw", [P, DenseFetch.CHUNKS, T], fp32, END - TOP)
    ctx_raw, _ = place("ctx_raw", [P, ContextFetch.RING, BANK], fp32, END - TOP)
    gu, _ = place("gu", [P, 2, 2, C, P], fp16, END - TOP)
    dw_raw, _ = place("dw_raw", [P, 2, C, P], fp32, END - 2 * TOP)
    t0, t1, x2t = [t0_hi, t0_lo], [t1_hi, t1_lo], [x2t_hi, x2t_lo]

    with ExitStack() as semaphores:
        def stage_semaphores(scope):
            return lambda name: scope.enter_context(nc.semaphore(name))

        sem = stage_semaphores(semaphores)
        dense_fetch = DenseFetch(sem, dw_raw, [dw_hi, dw_lo], a_raw, resid, (out_bias, query_bias, key_bias), {
            "dense": dense_w, "att_t": att_t, "x": x, "out_bias": out_bias_in, "query_bias": query_bias_in,
            "key_bias": key_bias_in})
        context_fetch = ContextFetch(sem, ctx_raw, [ctx_hi, ctx_lo], {"ctx": ctx})
        gate_up_fetch = GateUpFetch(sem, gu, {"gate_up": gate_up})
        y_early = attention(nc, sem, place, at_stages, at_t1, consts, qkv_bias, t0, dense_fetch,
                            {"x_t": x_t, "wqkv": wqkv, "dense": dense_w, "consts": consts_in,
                             "qkv_bias": qkv_bias_in, "att_t": att_t})
        dense(nc, sem, place, at_dense, dense_fetch, context_fetch, consts, y_early, out_bias, query_bias,
              key_bias, resid, t0, t1, shift, {"dense": dense_w, "att_t": att_t})
        cross(nc, sem, place, at_t0, at_cross, context_fetch, gate_up_fetch, x2t, consts, resid, t1, shift, {"ctx": ctx})
        ffn(nc, sem, place, at_t0, at_end, at_rings, gate_up_fetch, x2t, consts, resid,
            {"gate_up": gate_up, "down": down, "out": out})


def kernel(**inputs):
    import numpy as _np
    import concourse.bacc as _bacc
    from concourse import mybir as _mybir
    from concourse.bass_utils import run_bass_kernel_spmd as _run

    def array(name):
        return _np.asarray(inputs[name])

    def stationary(w):
        return w.reshape(w.shape[0] // P, P, C, P).transpose(0, 3, 2, 1)

    x, ctx = array("x"), array("ctx_4096")
    wk = array("L0_xattn_Wk").reshape(C, P, C, P).transpose(2, 1, 0, 3)
    gate_up = _np.stack([stationary(array("L0_ffn_W_gate")), stationary(array("L0_ffn_W_up"))], axis=2)
    ctx_t = ctx.transpose(0, 2, 1)
    streams = [a[b].reshape(C, P, HALVES, BANK).transpose(2, 0, 1, 3) for a in (ctx_t, ctx) for b in range(B)]

    eye = _np.eye(P, dtype=_np.float32)
    rows, cols = _np.arange(P)[:, None], _np.arange(P)[None, :]
    masked = _np.where(cols > rows, MASKED, 0.0)
    ramp = _np.broadcast_to(_np.arange(T) - (T - P), (P, T))
    slopes = 2.0 ** (-(_np.arange(H) + 1.0) * ALIBI_MAX / H) * float(HD) ** 0.5
    consts = _np.concatenate([eye, ramp, masked, _np.broadcast_to(_np.tile(slopes, B), (P, HEADS))], axis=1)

    laid_out = {
        "x_t": x.transpose(0, 2, 1).reshape(B, C, P, T),
        "x": x.reshape(B, TB, P, D),
        "ctx": _np.stack(streams).reshape(4 * B * C, P, BANK),
        "wqkv": array("L0_attn_w_qkv").reshape(3, NG, P, C, P).transpose(1, 0, 4, 3, 2).reshape(NG * 3, P, C * P),
        "dense": _np.concatenate([stationary(array("L0_attn_w_out")), stationary(array("L0_xattn_Wq")), wk]
                                 ).reshape(3 * C, P, C * P),
        "gate_up": gate_up.reshape(MB, P, 2 * C * P),
        "down": array("L0_ffn_W_down").T.reshape(MB // 2, 2, P, HALVES, BANK).transpose(3, 0, 2, 1, 4)
                .reshape(HALVES * MB // 2, P, 2 * BANK),
        "consts": consts.astype(_np.float32),
        "qkv_bias": _np.tile(array("L0_attn_b_qkv").reshape(3, NG, P).transpose(2, 0, 1), (1, 1, B)).reshape(P, 3 * UNITS),
        "out_bias": array("L0_attn_b_out").reshape(C, P).T,
        "query_bias": array("L0_xattn_bq").reshape(C, P).T,
        "key_bias": array("L0_xattn_bk").reshape(C, P).T,
    }
    nc = _bacc.Bacc("TRN2", target_bir_lowering=False, num_devices=1)
    arrays, args = {}, []
    for name, value in laid_out.items():
        value = _np.ascontiguousarray(value)
        arrays[f"in_{name}"] = value
        args.append(nc.dram_tensor(f"in_{name}", value.shape, _mybir.dt.from_np(value.dtype), kind="ExternalInput").ap())
    att_t = nc.dram_tensor("att_t_scratch", (UNITS, P, T), _mybir.dt.float32, kind="Internal").ap()
    out = nc.dram_tensor("out", (B, TB, P, D), _mybir.dt.float32, kind="ExternalOutput").ap()
    named = dict(zip(laid_out, args))
    decoder_layer(nc, named["x_t"], named["x"], named["ctx"], named["wqkv"], named["dense"], named["gate_up"],
                  named["down"], named["consts"], named["qkv_bias"], named["out_bias"], named["query_bias"],
                  named["key_bias"], att_t, out)
    result = _run(nc, [arrays], core_ids=[0])
    return result.results[0]["out"].reshape(B, T, D)
```
